# Optimizing a Trainium2 kernel written in Bass

```python
import numpy as np
import jax
import jax.numpy as jnp

def _softmax(x, axis=-1):
    return jax.nn.softmax(x, axis=axis)

def _gelu(x):
    return jax.nn.gelu(x, approximate=True)

def _silu(x):
    return jax.nn.silu(x)

def _sigmoid(x):
    return jax.nn.sigmoid(x)

def _layernorm(x, axis=-1, eps=1e-05):
    m = jnp.mean(x, axis=axis, keepdims=True)
    v = jnp.var(x, axis=axis, keepdims=True)
    return (x - m) / jnp.sqrt(v + eps)

def _scatter_add(tgt, idx, src, axis=0):
    return tgt.at[idx].add(src)

def _segment_sum(src, seg, n):
    return jax.ops.segment_sum(src, seg, n)
kernel_name = 'mk_xattn_ffn_d1_seqx_r4_ae64a7'

def setup_inputs(seed: int=0):
    np.random.seed(seed)
    _w = jnp.asarray

    def _rec_inputs():
        import jax
        import jax.numpy as jnp
        _rk = jax.random.key(seed)
        x = 2.818e-05 + 1 * jax.random.normal(jax.random.fold_in(_rk, 1), (4, 512, 512), jnp.float32)
        _lenS = 512 - jax.random.randint(jax.random.fold_in(_rk, 7), (4,), 0, max(1, 512 // 4) + 1, jnp.int32)
        _lenS2 = 512 - jax.random.randint(jax.random.fold_in(_rk, 8), (4,), 0, max(1, 512 // 4) + 1, jnp.int32)
        _ctx_1024P = jax.random.normal(jax.random.fold_in(_rk, 11), (4, 16, 256), jnp.float32)
        _ctx_1024c = jax.random.dirichlet(jax.random.fold_in(_rk, 511), 0.3 * jnp.ones((16,), jnp.float32), (4, 512))
        _ctx_1024t = jnp.einsum('bsk,bkd->bsd', _ctx_1024c, _ctx_1024P)
        _ctx_1024t = _ctx_1024t * jax.lax.rsqrt(jnp.mean(jnp.square(_ctx_1024t)) + 1e-12) * 0.953939
        ctx_1024 = 7.22013e-05 + 1.00017 * (_ctx_1024t + 0.3 * jax.random.normal(jax.random.fold_in(_rk, 611), (4, 512, 256), jnp.float32))
        return (x, ctx_1024)
    x, ctx_1024 = _rec_inputs()

    def _L0_xattn_setup():
        import jax, jax.numpy as jnp
        import numpy as np
        B_, L_, D_MODEL = (4, 512, 256)
        D_STATE, D_CONV, EXPAND = (16, 4, 2)
        D_INNER = EXPAND * D_MODEL
        DT_RANK = (D_MODEL + 15) // 16

        def silu(x):
            return x * jax.nn.sigmoid(x)
        key = jax.random.key(seed)
        ks = jax.random.split(key, 10)
        f32 = jnp.float32
        hidden_states = jax.random.normal(ks[0], (B_, L_, D_MODEL), dtype=f32)
        z = jax.random.normal(ks[1], (B_, D_INNER, L_), dtype=f32)
        in_proj_w = jax.random.normal(ks[2], (D_INNER, D_MODEL), dtype=f32) * 0.02
        conv_w = jax.random.normal(ks[3], (D_INNER, 1, D_CONV), dtype=f32) * 0.1
        conv_b = jax.random.normal(ks[4], (D_INNER,), dtype=f32) * 0.02
        x_proj_w = jax.random.normal(ks[5], (DT_RANK + 2 * D_STATE, D_INNER), dtype=f32) * 0.02
        dt_proj_w = jax.random.uniform(ks[6], (D_INNER, DT_RANK), dtype=f32, minval=-DT_RANK ** (-0.5), maxval=DT_RANK ** (-0.5))
        dt = jnp.exp(jax.random.uniform(ks[7], (D_INNER,), dtype=f32, minval=np.log(0.001), maxval=np.log(0.1)))
        dt_proj_b = jnp.log(jnp.expm1(dt))
        A_log = jnp.log(jnp.broadcast_to(jnp.arange(1, D_STATE + 1, dtype=f32), (D_INNER, D_STATE)))
        D = jnp.ones((D_INNER,), f32)
        return {'hidden_states': hidden_states, 'z': z, 'in_proj_w': in_proj_w, 'conv_w': conv_w, 'conv_b': conv_b, 'x_proj_w': x_proj_w, 'dt_proj_w': dt_proj_w, 'dt_proj_b': dt_proj_b, 'A_log': A_log, 'D': D}
    _L0_xattn_all = _L0_xattn_setup()
    _L0_xattn_in = {k: v for k, v in _L0_xattn_all.items() if k in ('in_proj_w', 'conv_w', 'conv_b', 'x_proj_w', 'dt_proj_w', 'dt_proj_b', 'A_log', 'D')}
    del _L0_xattn_all

    def _L0_ffn_setup():
        import math
        import jax, jax.numpy as jnp
        import numpy as np
        DIM = 512
        RANK = 8
        B, T = (4, 1024)

        def _orthogonal(key, n):
            a = jax.random.normal(key, (n, n), dtype=jnp.float32)
            q, r = jnp.linalg.qr(a)
            q = q * jnp.sign(jnp.diagonal(r))[None, :]
            return q
        key = jax.random.key(seed)
        kx, kf = jax.random.split(key)
        x = jax.random.normal(kx, (B, T, DIM), dtype=jnp.float32)
        fkeys = jax.random.split(kf, RANK)
        factors = jnp.stack([_orthogonal(fkeys[r], DIM) * (r + 1) ** (-0.5) for r in range(RANK)])
        bias = jnp.zeros((DIM,), dtype=jnp.float32)
        return {'x': x, 'factors': factors, 'bias': bias}
    _L0_ffn_all = _L0_ffn_setup()
    _L0_ffn_in = {k: v for k, v in _L0_ffn_all.items() if k in ('factors', 'bias')}
    del _L0_ffn_all
    return {'x': x, 'ctx_1024': ctx_1024, 'L0_xattn_in_proj_w': _L0_xattn_in['in_proj_w'], 'L0_xattn_conv_w': _L0_xattn_in['conv_w'], 'L0_xattn_conv_b': _L0_xattn_in['conv_b'], 'L0_xattn_x_proj_w': _L0_xattn_in['x_proj_w'], 'L0_xattn_dt_proj_w': _L0_xattn_in['dt_proj_w'], 'L0_xattn_dt_proj_b': _L0_xattn_in['dt_proj_b'], 'L0_xattn_A_log': _L0_xattn_in['A_log'], 'L0_xattn_D': _L0_xattn_in['D'], 'L0_ffn_factors': _L0_ffn_in['factors'], 'L0_ffn_bias': _L0_ffn_in['bias']}

def reference(x, ctx_1024, L0_xattn_in_proj_w, L0_xattn_conv_w, L0_xattn_conv_b, L0_xattn_x_proj_w, L0_xattn_dt_proj_w, L0_xattn_dt_proj_b, L0_xattn_A_log, L0_xattn_D, L0_ffn_factors, L0_ffn_bias):
    import jax
    import jax.numpy as jnp

    def _L0_xattn_ref(hidden_states, z, in_proj_w, conv_w, conv_b, x_proj_w, dt_proj_w, dt_proj_b, A_log, D):
        import jax, jax.numpy as jnp
        import numpy as np
        B_, L_, D_MODEL = (4, 512, 256)
        D_STATE, D_CONV, EXPAND = (16, 4, 2)
        D_INNER = EXPAND * D_MODEL
        DT_RANK = (D_MODEL + 15) // 16

        def silu(x):
            return x * jax.nn.sigmoid(x)
        Bsz, L, _ = hidden_states.shape
        d_inner, _, d_conv = conv_w.shape
        dt_rank = dt_proj_w.shape[1]
        d_state = A_log.shape[1]
        x = jnp.einsum('bld,ed->bel', hidden_states, in_proj_w)
        xc = jax.lax.conv_general_dilated(x, conv_w, window_strides=(1,), padding=[(d_conv - 1, 0)], feature_group_count=d_inner, dimension_numbers=('NCH', 'OIH', 'NCH'))
        x = silu(xc + conv_b[None, :, None])
        x_dbl = jnp.einsum('bdl,ed->bel', x, x_proj_w)
        dt_low, Bm, Cm = jnp.split(x_dbl, [dt_rank, dt_rank + d_state], axis=1)
        dt = jnp.einsum('brl,dr->bdl', dt_low, dt_proj_w)
        dt = jax.nn.softplus(dt + dt_proj_b[None, :, None])
        A = -jnp.exp(A_log)
        dt_t = jnp.moveaxis(dt, -1, 0)
        B_t = jnp.moveaxis(Bm, -1, 0)
        C_t = jnp.moveaxis(Cm, -1, 0)
        u_t = jnp.moveaxis(x, -1, 0)

        def step(state, inp):
            d, b, c, u = inp
            dA = jnp.exp(d[..., None] * A)
            state = state * dA + (d * u)[..., None] * b[:, None, :]
            y = jnp.einsum('bdn,bn->bd', state, c)
            return (state, y)
        state0 = jnp.zeros((Bsz, d_inner, d_state), x.dtype)
        _, ys = jax.lax.scan(step, state0, (dt_t, B_t, C_t, u_t))
        y = jnp.moveaxis(ys, 0, 2)
        y = y + D[None, :, None] * x
        y = y * silu(z)
        return jnp.swapaxes(y, 1, 2)

    def _L0_ffn_ref(x, factors, bias):
        import math
        import jax, jax.numpy as jnp
        import numpy as np
        DIM = 512
        RANK = 8
        B, T = (4, 1024)

        def _orthogonal(key, n):
            a = jax.random.normal(key, (n, n), dtype=jnp.float32)
            q, r = jnp.linalg.qr(a)
            q = q * jnp.sign(jnp.diagonal(r))[None, :]
            return q
        rank = factors.shape[0]
        mixed = jnp.einsum('btd,rde->bte', x, factors)
        mixed = mixed / math.sqrt(rank) + bias
        return mixed
    x = x + _L0_xattn_ref(ctx_1024, _layernorm(x, axis=-1), L0_xattn_in_proj_w, L0_xattn_conv_w, L0_xattn_conv_b, L0_xattn_x_proj_w, L0_xattn_dt_proj_w, L0_xattn_dt_proj_b, L0_xattn_A_log, L0_xattn_D)
    x = x + _L0_ffn_ref(_layernorm(x, axis=-1), L0_ffn_factors, L0_ffn_bias)
    return x

_drawn_inputs = setup_inputs


def setup_inputs(seed=0):
    import zlib

    import numpy as np

    out = dict(_drawn_inputs(seed))
    spreads = {'L0_xattn_D': (1.0, 0.6), 'L0_ffn_bias': (0.0, 0.8)}
    factors = {'ctx_1024': 2.91,
     'L0_xattn_in_proj_w': 2.912,
     'L0_xattn_conv_w': 2.966,
     'L0_xattn_conv_b': 8.0,
     'L0_xattn_x_proj_w': 8.0,
     'L0_xattn_dt_proj_w': 8.0,
     'L0_xattn_dt_proj_b': 8.0,
     'L0_xattn_A_log': 8.0,
     'L0_ffn_factors': 8.0}
    for name, (base, spread) in spreads.items():
        noise = np.random.default_rng([zlib.crc32(name.encode()), seed]).standard_normal(out[name].shape)
        drawn = base * np.exp(spread * noise) if base else spread * noise
        out[name] = jnp.asarray(drawn.astype(out[name].dtype))
    for name, factor in factors.items():
        out[name] = (out[name] * factor).astype(out[name].dtype)
    return out
```

```python
from contextlib import ExitStack

import concourse.bass as bass
from concourse import mybir

ALU = mybir.AluOpType
ACT = mybir.ActivationFunctionType
F32 = mybir.dt.float32
U32 = mybir.dt.uint32

P = 128
BATCH, L, DM = 4, 512, 256
DI, N, TAPS, RANK = 512, 16, 4, 16
KB = DI // P
CB = DM // P
FR = 8
PAIRS = N // 2
STEPS = BATCH * KB
EPS = 1e-5
H_RING = 4
BC_ROW = 32
POLY_BELOW = 2.0 ** -7
SQ_SCALE = 3.0 ** -0.5


def build(nc, x, ctxT, w_inT, channel, x_projT, dt_wT, factors, bias, out):
    bc_dram = nc.dram_tensor("bc_scratch", (BATCH, 2 * N, L), F32, kind="Internal").ap()

    with ExitStack() as ctx:
        def sb(name, shape, dt=F32):
            return ctx.enter_context(nc.sbuf_tensor(name, shape, dt))

        def ps(name, shape):
            return ctx.enter_context(nc.psum_tensor(name, shape, F32))

        def sem(name):
            return ctx.enter_context(nc.semaphore(name))

        ident = sb("ident", [P, P])
        diag_d = sb("diag_d", [P, KB, P])
        ones_row = sb("ones_row", [P, P])
        bias_row = sb("bias_row", [P, DI])
        w_in = sb("w_in", [P, CB, DI])
        chan = sb("chan", [P, KB, TAPS + 2 + N])
        cw = chan[:, :, 0:TAPS]
        cb = chan[:, :, TAPS]
        dsk = chan[:, :, TAPS + 1]
        a_log = chan[:, :, TAPS + 2:]
        w_x = sb("w_x", [P, KB, P])
        w_dt = sb("w_dt", [P, DI])
        a_neg = sb("a_neg", [P, KB, N])
        fsum = sb("fsum", [P, KB, DI])
        ctx_sb = sb("ctx_sb", [P, CB, L])
        x1 = sb("x1", [P, BATCH * KB * DI])
        b_rep = sb("b_rep", [P, PAIRS, 2, L])
        c_rep = sb("c_rep", [P, PAIRS, 2, L])
        bc = sb("bc", [2 * N + BC_ROW, L])
        dt_low = sb("dt_low", [P, L])
        u = sb("u", [P, KB, L])
        acc = sb("acc", [P, 2, L])
        ut = sb("ut", [P, 2, L])
        gate = sb("gate", [P, KB, L])
        gt = sb("gt", [P, 2, L])
        g_stat = sb("g_stat", [P, 6])
        g_mv = sb("g_mv", [P, 2])
        g_r = sb("g_r", [P, 6])
        e_dt = sb("e_dt", [P, L])
        l_dt = sb("l_dt", [P, L])
        q_dt = sb("q_dt", [P, L])
        m_dt = sb("m_dt", [P, L], U32)
        dt = sb("dt", [P, 2, L])
        dtu = sb("dtu", [P, 2, L])
        dbu = sb("dbu", [P, 2, 2, L])
        h = sb("h", [P, H_RING, 2, L])
        yg = sb("yg", [P, L])
        xn = sb("xn", [P, DI])
        xnT = sb("xnT", [P, KB, P])
        t_stat = sb("t_stat", [P, 6])
        t_mv = sb("t_mv", [P, 2])
        t_r = sb("t_r", [P, 6])
        cols = sb("cols", [P, 2])
        eps_col, sq_col = cols[:, 0:1], cols[:, 1:2]

        dA = ps("dA", [P, 2, 2, L])
        y = [ps(f"y{i}", [P, L]) for i in range(2)]
        work0 = ps("work0", [P, L])
        work1 = ps("work1", [P, L])

        w_in_landed, w_x_landed, w_dt_landed, bias_landed, ch_landed = (
            sem(f"{n}_landed") for n in ("w_in", "w_x", "w_dt", "bias", "ch"))
        ctx_landed = sem("ctx_landed")
        x_landed = sem("x_landed")
        ident_zero = sem("ident_zero")
        ident_ready = sem("ident_ready")
        pads_ready = sem("pads_ready")
        da_zero = sem("da_zero")
        diag_ready = sem("diag_ready")
        a_exp = sem("a_exp")
        a_ready = sem("a_ready")
        f_landed = sem("f_landed")
        f_scaled = sem("f_scaled")
        in_mm = sem("in_mm")
        tap = sem("tap")
        conv = sem("conv")
        u_abs, u_exp, u_ln, u_arg, u_sig, u_done = (sem(f"u_{n}") for n in ("abs", "exp", "ln", "arg", "sig", "done"))
        g_bn, g_aggr, g_lnv, g_expv, g_newton, g_zn = (
            sem(f"g_{n}") for n in ("bn", "aggr", "lnv", "expv", "newton", "zn"))
        g_abs, g_exp, g_ln, g_arg, g_sig, g_done = (sem(f"g_{n}") for n in ("abs", "exp", "ln", "arg", "sig", "done"))
        x_mm = sem("x_mm")
        bc_evac = sem("bc_evac")
        dtl_evac = sem("dtl_evac")
        bc_stored = sem("bc_stored")
        b_landed = [sem(f"b_landed{j}") for j in range(PAIRS)]
        c_landed = [sem(f"c_landed{j}") for j in range(PAIRS)]
        d_mm, d_abs, d_exp, d_ln, d_sq, d_poly, d_mask, d_sel, d_dt, d_dtu = (
            sem(f"d_{n}") for n in ("mm", "abs", "exp", "ln", "sq", "poly", "mask", "sel", "dt", "dtu"))
        y_init = sem("y_init")
        exp_done = sem("exp_done")
        mulb = sem("mulb")
        scanned = sem("scanned")
        mulc = sem("mulc")
        summed = sem("summed")
        gated = sem("gated")
        y_turned = sem("y_turned")
        x1_added = sem("x1_added")
        t_bn, t_aggr, t_lnv, t_expv, t_newton, t_xn, t_turned, t_xnT, t_ffn, t_final = (
            sem(f"t_{n}") for n in ("bn", "aggr", "lnv", "expv", "newton", "xn", "turned", "xnT", "ffn", "final"))
        out_stored = sem("out_stored")

        def x1_block(b, k):
            return x1[:, bass.ds(b * (KB * DI) + k * DI, DI)]

        def x1_columns(b, k):
            return x1[:, bass.ds(b * (KB * DI), KB * DI)].rearrange("p (t d) -> p t d", t=KB)[:, :, k * P:(k + 1) * P]

        block = ctx.enter_context(nc.Block())

        @block.sync
        def _(sp):
            sp.dma_start(ctx_sb[:], ctxT[:, 0, :].rearrange("(c p) l -> p c l", p=P)).then_inc(ctx_landed, 16)
            sp.dma_start(w_in[:], w_inT.rearrange("(c p) e -> p c e", p=P)).then_inc(w_in_landed, 16)
            sp.dma_start(chan[:], channel.rearrange("(k p) t -> p k t", p=P)).then_inc(ch_landed, 16)
            sp.dma_start(w_x[:, :, 0:2 * N + BC_ROW], x_projT.rearrange("(k p) e -> p k e", p=P)).then_inc(w_x_landed, 16)
            sp.wait_ge(pads_ready, 1)
            sp.dma_start(w_dt[0:RANK + 1, :], dt_wT).then_inc(w_dt_landed, 16)
            sp.dma_start(bias_row[0:1, :], bias).then_inc(bias_landed, 16)
            sp.dma_start(x1[:, 0:KB * DI].rearrange("p (t d) -> p t d", t=KB),
                         x[0].rearrange("(t p) d -> p t d", p=P)).then_inc(x_landed, 16)
            sp.wait_ge(in_mm, KB)
            sp.wait_ge(ctx_landed, 16)
            sp.dma_start(ctx_sb[:], ctxT[:, 1, :].rearrange("(c p) l -> p c l", p=P)).then_inc(ctx_landed, 16)

            def spread_bc(b):
                sp.wait_ge(bc_evac, b + 1)
                sp.dma_start(bc_dram[bass.ds(b, 1)].rearrange("b n l -> (b n) l"),
                             bc[BC_ROW:BC_ROW + 2 * N, :]).then_inc(bc_stored, 16)
                sp.wait_ge(bc_stored, (b + 1) * 16)
                rows = bc_dram[bass.ds(b, 1)].rearrange("b n l -> b (n l)")
                for j in range(PAIRS):
                    if not (isinstance(b, int) and b == 0):
                        sp.wait_ge(mulb, b * (KB * PAIRS) - PAIRS + j + 1)
                    sp.dma_start(b_rep[:, j].rearrange("p i l -> p (i l)"),
                                 rows[:, 2 * j * L:(2 * j + 2) * L].to_broadcast([P, 2 * L])).then_inc(b_landed[j], 16)
                    if not (isinstance(b, int) and b == 0):
                        sp.wait_ge(mulc, b * (KB * PAIRS) - PAIRS + j + 1)
                    sp.dma_start(c_rep[:, j].rearrange("p i l -> p (i l)"),
                                 rows[:, (N + 2 * j) * L:(N + 2 * j + 2) * L].to_broadcast([P, 2 * L])
                                 ).then_inc(c_landed[j], 16)

            def store(b, k):
                sp.wait_ge(t_final, b * KB + k + 1)
                sp.dma_start(out[bass.ds(b, 1), k * P:(k + 1) * P, :].rearrange("b p d -> (b p) d"),
                             x1_block(b, k)).then_inc(out_stored, 16)

            def batch(b, first, last, more_ctx):
                if not last:
                    sp.wait_ge(x_landed, (b + 1) * 16)
                    sp.dma_start(x1[:, bass.ds((b + 1) * (KB * DI), KB * DI)].rearrange("p (t d) -> p t d", t=KB),
                                 x[bass.ds(b + 1, 1)].rearrange("b (t p) d -> p (b t) d", p=P)).then_inc(x_landed, 16)
                if not first:
                    for k in range(KB - 1):
                        store(b - 1, k)
                if not last:
                    if more_ctx:
                        sp.wait_ge(in_mm, (b + 2) * KB)
                        sp.wait_ge(ctx_landed, (b + 2) * 16)
                        sp.dma_start(ctx_sb[:], ctxT[:, bass.ds(b + 2, 1), :].rearrange("(c p) b l -> p c (b l)", p=P)
                                     ).then_inc(ctx_landed, 16)
                    spread_bc(b + 1)
                if not first:
                    store(b - 1, KB - 1)

            spread_bc(0)
            batch(0, True, False, True)
            batch(1, False, False, True)
            batch(2, False, False, False)
            batch(3, False, True, False)
            for k in range(KB):
                store(BATCH - 1, k)
            sp.wait_ge(out_stored, STEPS * 16)

        @block.tensor
        def _(pe):
            def in_proj(bank, s, k):
                for c in range(CB):
                    mm = pe.matmul(bank[:], w_in[:, c, k * P:(k + 1) * P], ctx_sb[:, c, :],
                                   start=(c == 0), stop=(c == CB - 1))
                mm.then_inc(in_mm, 1)

            def x_proj(ks):
                for k in ks:
                    mm = pe.matmul(work0[:], w_x[:, k, :], u[:, k, :], start=(k == 0), stop=(k == KB - 1),
                                   skip_group_check=True)
                if KB - 1 in ks:
                    mm.then_inc(x_mm, 1)

            def dt_proj(k):
                pe.matmul(work0[:], w_dt[:, k * P:(k + 1) * P], dt_low[:], start=True, stop=True).then_inc(d_mm, 1)

            def turn_y(s):
                pe.wait_ge(gated, s + 1)
                for t in range(KB):
                    tr = pe.transpose(work1[:, t * P:(t + 1) * P], yg[:, t * P:(t + 1) * P], ident[:])
                tr.then_inc(y_turned, 1)

            def turn_xn(t):
                pe.wait_ge(t_xn, t + 1)
                for k in range(KB):
                    tr = pe.transpose(work1[:, k * P:(k + 1) * P], xn[:, k * P:(k + 1) * P], ident[:])
                tr.then_inc(t_turned, 1)

            def last_layer(t):
                pe.wait_ge(t_xnT, t + 1)
                for k in range(KB):
                    pe.matmul(work1[:], xnT[:, k, :], fsum[:, k, :], start=(k == 0), stop=False)
                pe.matmul(work1[:], ones_row[:], bias_row[:], start=False, stop=True).then_inc(t_ffn, 1)

            def state_sum(s, k, j):
                pe.wait_ge(mulc, s * PAIRS + j + 1)
                for i in range(2):
                    mm = pe.matmul(y[k % 2][:], ident[:], h[:, j % H_RING, i, :], start=False,
                                   stop=(j == PAIRS - 1 and i == 1))
                mm.then_inc(summed, 1)

            def step(b, k, first, last):
                s = b * KB + k
                for j in range(PAIRS):
                    if j == 0:
                        pe.wait_ge(u_done, s + 1)
                        if not (first and k < 2):
                            pe.wait_ge(gated, s - 1)
                        pe.matmul(y[k % 2][:], diag_d[:, k, :], u[:, k, :], start=True, stop=False).then_inc(y_init, 1)
                        if not last:
                            pe.wait_ge(d_dt, s + 1)
                            pe.wait_ge(ctx_landed, (b + 2) * 16)
                            in_proj(work0, s + KB, k)
                    if j == 1 and not (first and k == 0):
                        if not first and not (isinstance(b, int) and b == 1 and k == 0):
                            pe.wait_ge(t_final, s - KB)
                        turn_y(s - 1)
                    if j == 3 and k == KB - 1 and not last:
                        pe.wait_ge(tap, s + KB + 1)
                        pe.wait_ge(conv, (s + KB + 1) * 3)
                        x_proj(range(KB - 1))
                    if j == 4 and k < KB - 1:
                        if not last:
                            pe.wait_ge(tap, s + KB + 1)
                            pe.wait_ge(conv, (s + KB + 1) * 3)
                        else:
                            pe.wait_ge(d_dt, s + 1)
                        dt_proj(k + 1)
                    if j == 5:
                        if not first:
                            pe.wait_ge(x1_added, s)
                            turn_xn(s - KB)
                        if k == KB - 1 and not last:
                            pe.wait_ge(u_done, s + KB + 1)
                            x_proj([KB - 1])
                    if j == 6:
                        if k == KB - 1 and not last:
                            pe.wait_ge(bc_evac, b + 2)
                            pe.wait_ge(dtl_evac, b + 2)
                            dt_proj(0)
                        if not first:
                            last_layer(s - KB)
                    if j > 0:
                        state_sum(s, k, j - 1)
                state_sum(s, k, PAIRS - 1)

            banks = [work0, work1, y[0], y[1]]
            pe.wait_ge(ctx_landed, 16)
            pe.wait_ge(w_in_landed, 16)
            for k in range(KB):
                in_proj(banks[k], k, k)
            pe.wait_ge(w_x_landed, 16)
            pe.wait_ge(pads_ready, 1)
            pe.wait_ge(conv, 3)
            for k in range(KB):
                pe.wait_ge(u_done, k + 1)
                x_proj([k])
            pe.wait_ge(w_dt_landed, 16)
            pe.wait_ge(bc_evac, 1)
            pe.wait_ge(dtl_evac, 1)
            dt_proj(0)
            pe.wait_ge(ident_ready, 1)
            pe.wait_ge(diag_ready, KB)
            pe.wait_ge(conv, 3 * KB)
            for k in range(KB):
                step(0, k, True, False)
            pe.wait_ge(f_scaled, 1)
            pe.wait_ge(bias_landed, 16)
            for b in range(1, BATCH):
                for k in range(KB):
                    step(b, k, False, b == BATCH - 1)
            pe.wait_ge(t_final, STEPS - KB)
            turn_y(STEPS - 1)
            for t in range(STEPS - KB, STEPS):
                if t == STEPS - KB:
                    pe.wait_ge(x1_added, STEPS)
                else:
                    pe.wait_ge(t_final, t)
                turn_xn(t)
                last_layer(t)

        @block.scalar
        def _(act):
            def conv_tap(bank, n, k):
                act.wait_ge(in_mm, n + 1)
                if not (isinstance(n, int) and n < 2):
                    act.wait_ge(u_done, n - 1)
                act.activation(acc[:, k % 2, :], bank[:], ACT.Identity, bias=cb[:, k:k + 1],
                               scale=cw[:, k, TAPS - 1:TAPS]).then_inc(tap, 1)

            def u_abs_(n, k):
                act.wait_ge(conv, n * 3 + 3)
                act.activation(ut[:, k % 2, :], acc[:, k % 2, :], ACT.Abs).then_inc(u_abs, 1)

            def u_exp_(n, k):
                act.wait_ge(u_abs, n + 1)
                act.activation(ut[:, k % 2, :], ut[:, k % 2, :], ACT.Exp, scale=-1.0).then_inc(u_exp, 1)

            def u_ln_(n, k):
                act.wait_ge(u_exp, n + 1)
                act.activation(ut[:, k % 2, :], ut[:, k % 2, :], ACT.Ln, bias=1.0).then_inc(u_ln, 1)

            def u_sig_(n, k):
                act.wait_ge(u_arg, n + 1)
                act.activation(ut[:, k % 2, :], ut[:, k % 2, :], ACT.Exp).then_inc(u_sig, 1)

            def g_lnv_(n):
                act.wait_ge(g_aggr, n + 1)
                act.activation(g_r[:, 0:1], g_mv[:, 1:2], ACT.Ln, bias=eps_col).then_inc(g_lnv, 1)

            def g_expv_(n):
                act.wait_ge(g_lnv, n + 1)
                act.activation(g_r[:, 1:2], g_r[:, 0:1], ACT.Exp, scale=-0.5).then_inc(g_expv, 1)

            def g_zn_(b, k, n):
                act.wait_ge(g_newton, n * 4 + 4)
                act.activation(gate[:, k, :], x1_block(b, k), ACT.Identity, bias=g_r[:, 5:6],
                               scale=g_r[:, 4:5]).then_inc(g_zn, 1)

            def g_abs_(n, k):
                act.wait_ge(g_zn, n + 1)
                if not (isinstance(n, int) and n < 2):
                    act.wait_ge(g_done, n - 1)
                act.activation(gt[:, k % 2, :], gate[:, k, :], ACT.Abs).then_inc(g_abs, 1)

            def g_exp_(n, k):
                act.wait_ge(g_abs, n + 1)
                act.activation(gt[:, k % 2, :], gt[:, k % 2, :], ACT.Exp, scale=-1.0).then_inc(g_exp, 1)

            def g_ln_(n, k):
                act.wait_ge(g_exp, n + 1)
                act.activation(gt[:, k % 2, :], gt[:, k % 2, :], ACT.Ln, bias=1.0).then_inc(g_ln, 1)

            def g_sig_(n, k):
                act.wait_ge(g_arg, n + 1)
                act.activation(gt[:, k % 2, :], gt[:, k % 2, :], ACT.Exp).then_inc(g_sig, 1)

            def x_evac(b):
                act.wait_ge(x_mm, b + 1)
                if not (isinstance(b, int) and b == 0):
                    act.wait_ge(bc_stored, b * 16)
                    act.wait_ge(d_mm, b * KB)
                act.activation(bc[BC_ROW:BC_ROW + 2 * N, :], work0[BC_ROW:BC_ROW + 2 * N, :], ACT.Copy
                               ).then_inc(bc_evac, 1)
                act.activation(dt_low[0:RANK, :], work0[0:RANK, :], ACT.Copy).then_inc(dtl_evac, 1)

            def d_abs_(n):
                act.wait_ge(d_mm, n + 1)
                if not (isinstance(n, int) and n == 0):
                    act.wait_ge(d_dt, n)
                act.activation(e_dt[:], work0[:], ACT.Abs).then_inc(d_abs, 1)

            def d_exp_(n):
                act.wait_ge(d_abs, n + 1)
                act.activation(e_dt[:], e_dt[:], ACT.Exp, scale=-1.0).then_inc(d_exp, 1)

            def d_ln_(n):
                act.wait_ge(d_exp, n + 1)
                act.activation(l_dt[:], e_dt[:], ACT.Ln, bias=1.0).then_inc(d_ln, 1)

            def d_sq_(n):
                act.activation(q_dt[:], e_dt[:], ACT.Square, scale=SQ_SCALE, bias=sq_col).then_inc(d_sq, 1)

            def t_lnv_(t):
                act.wait_ge(t_aggr, t + 1)
                act.activation(t_r[:, 0:1], t_mv[:, 1:2], ACT.Ln, bias=eps_col).then_inc(t_lnv, 1)

            def t_expv_(t):
                act.wait_ge(t_lnv, t + 1)
                act.activation(t_r[:, 1:2], t_r[:, 0:1], ACT.Exp, scale=-0.5).then_inc(t_expv, 1)

            def t_xn_(b, k, t):
                act.wait_ge(t_newton, t * 4 + 4)
                if not (isinstance(t, int) and t == 0):
                    act.wait_ge(t_turned, t)
                act.activation(xn[:], x1_block(b, k), ACT.Identity, bias=t_r[:, 5:6], scale=t_r[:, 4:5]
                               ).then_inc(t_xn, 1)

            def t_xnT_(t):
                act.wait_ge(t_turned, t + 1)
                if not (isinstance(t, int) and t == 0):
                    act.wait_ge(t_ffn, t)
                act.activation(xnT[:].rearrange("p k l -> p (k l)"), work1[:], ACT.Copy).then_inc(t_xnT, 1)

            def decay(s, k, j, i):
                act.activation(dA[:, j % 2, i, 1:L], dt[:, k % 2, 1:L], ACT.Exp,
                               scale=a_neg[:, k, 2 * j + i:2 * j + i + 1]).then_inc(exp_done, 1)

            def step(b, k, first, last):
                s = b * KB + k
                kg = (k + KB - 1) % KB
                ng = s + KB - 1
                bg = b if k == 0 else b + 1
                gates = not last or k == 0
                tail = not first
                act.wait_ge(d_dt, s + 1)
                for j in range(PAIRS):
                    if j == 1 and gates:
                        g_lnv_(ng)
                    if j == 2 and not last:
                        u_abs_(s + KB, k)
                    if j == 3 and not last:
                        u_ln_(s + KB, k)
                    if j == 4:
                        if tail:
                            t_expv_(s - KB)
                        if not last:
                            u_sig_(s + KB, k)
                    if j == 5:
                        if gates:
                            g_abs_(ng, kg)
                        if k < KB - 1:
                            d_abs_(s + 1)
                    if j == 6:
                        if k < KB - 1:
                            d_exp_(s + 1)
                        if gates:
                            g_exp_(ng, kg)
                    if j == 7 and gates:
                        g_sig_(ng, kg)
                    if not (first and k == 0 and j < 2):
                        act.wait_ge(scanned, s * PAIRS + j - 1)
                    decay(s, k, j, 0)
                    if j == 0 and not last:
                        conv_tap(work0, s + KB, k)
                    if j == 1 and gates:
                        g_expv_(ng)
                    if j == 2 and not last:
                        u_exp_(s + KB, k)
                    if j == 3:
                        if gates:
                            if not (first and k == 0):
                                act.wait_ge(gated, s)
                            g_zn_(bg, kg, ng)
                        if tail:
                            t_lnv_(s - KB)
                    if j == 4 and tail:
                        t_xn_(b - 1, k, s - KB)
                    if j == 5:
                        if tail:
                            t_xnT_(s - KB)
                        if k == KB - 1 and not last:
                            x_evac(b + 1)
                    if j == 6:
                        if k < KB - 1:
                            d_ln_(s + 1)
                            d_sq_(s + 1)
                        elif not last:
                            d_abs_(s + 1)
                        if gates:
                            g_ln_(ng, kg)
                    if j == 7 and k == KB - 1 and not last:
                        d_exp_(s + 1)
                    decay(s, k, j, 1)
                    if j == 4 and first and k == 2:
                        act.wait_ge(f_landed, FR * 16)
                        act.activation(fsum[:], fsum[:], ACT.Copy, scale=FR ** -0.5).then_inc(f_scaled, 1)
                if k == KB - 1 and not last:
                    d_ln_(s + 1)
                    d_sq_(s + 1)

            act.preload_act_table_set("natural_log_exp_and_others")
            banks = [work0, work1, y[0], y[1]]
            act.wait_ge(ch_landed, 16)
            act.wait_ge(pads_ready, 1)
            for k in range(KB):
                conv_tap(banks[k], k, k)
                u_abs_(k, k)
                u_exp_(k, k)
                u_ln_(k, k)
                u_sig_(k, k)
            x_evac(0)
            d_abs_(0)
            d_exp_(0)
            d_ln_(0)
            d_sq_(0)
            act.activation(a_neg[:], a_log, ACT.Exp).then_inc(a_exp, 1)
            act.wait_ge(a_exp, 1)
            act.activation(a_neg[:], a_neg[:], ACT.Copy, scale=-1.0).then_inc(a_ready, 1)
            act.wait_ge(x_landed, 16)
            for k in range(KB - 1):
                g_lnv_(k)
                g_expv_(k)
                g_zn_(0, k, k)
                g_abs_(k, k)
                g_exp_(k, k)
                g_ln_(k, k)
                g_sig_(k, k)
            act.wait_ge(a_ready, 1)
            act.wait_ge(da_zero, 1)
            for b in range(BATCH):
                for k in range(KB):
                    step(b, k, b == 0, b == BATCH - 1)
            for k in range(KB):
                t = STEPS - KB + k
                t_lnv_(t)
                t_expv_(t)
                t_xn_(BATCH - 1, k, t)
                t_xnT_(t)

        @block.vector
        def _(dve):
            def conv_rest(bank, n, k):
                for i in range(1, TAPS):
                    if i == 1:
                        dve.wait_ge(tap, n + 1)
                    else:
                        dve.wait_ge(conv, n * 3 + i - 1)
                    dve.scalar_tensor_tensor(out=acc[:, k % 2, i:L], in0=bank[:, 0:L - i],
                                             scalar=cw[:, k, TAPS - 1 - i:TAPS - i], in1=acc[:, k % 2, i:L],
                                             op0=ALU.mult, op1=ALU.add).then_inc(conv, 1)

            def u_arg_(n, k):
                dve.wait_ge(u_ln, n + 1)
                dve.scalar_tensor_tensor(out=ut[:, k % 2, :], in0=acc[:, k % 2, :], scalar=0.0, in1=ut[:, k % 2, :],
                                         op0=ALU.min, op1=ALU.subtract).then_inc(u_arg, 1)

            def g_stats(b, k, n):
                if not (isinstance(n, int) and n == 0):
                    dve.wait_ge(g_zn, n)
                dve.bn_stats(g_stat[:], x1_block(b, k)).then_inc(g_bn, 1)
                dve.wait_ge(g_bn, n + 1)
                dve.bn_aggr(g_mv[:], g_stat[:]).then_inc(g_aggr, 1)

            def refine(r, mv, done, n):
                dve.scalar_tensor_tensor(out=r[:, 2:3], in0=mv[:, 1:2], scalar=EPS, in1=r[:, 1:2],
                                         op0=ALU.add, op1=ALU.mult).then_inc(done, 1)
                dve.wait_ge(done, n * 4 + 1)
                dve.scalar_tensor_tensor(out=r[:, 3:4], in0=r[:, 2:3], scalar=-0.5, in1=r[:, 1:2],
                                         op0=ALU.mult, op1=ALU.mult).then_inc(done, 1)
                dve.wait_ge(done, n * 4 + 2)
                dve.scalar_tensor_tensor(out=r[:, 4:5], in0=r[:, 3:4], scalar=1.5, in1=r[:, 1:2],
                                         op0=ALU.add, op1=ALU.mult).then_inc(done, 1)
                dve.wait_ge(done, n * 4 + 3)
                dve.scalar_tensor_tensor(out=r[:, 5:6], in0=mv[:, 0:1], scalar=-1.0, in1=r[:, 4:5],
                                         op0=ALU.mult, op1=ALU.mult).then_inc(done, 1)

            def g_refine(n):
                dve.wait_ge(g_expv, n + 1)
                refine(g_r, g_mv, g_newton, n)

            def g_arg_(n, k):
                dve.wait_ge(g_ln, n + 1)
                dve.scalar_tensor_tensor(out=gt[:, k % 2, :], in0=gate[:, k, :], scalar=0.0, in1=gt[:, k % 2, :],
                                         op0=ALU.min, op1=ALU.subtract).then_inc(g_arg, 1)

            def softplus(n, k):
                dve.wait_ge(d_exp, n + 1)
                dve.tensor_scalar(m_dt[:], e_dt[:], POLY_BELOW, None, ALU.is_ge).then_inc(d_mask, 1)
                dve.wait_ge(d_sq, n + 1)
                dve.scalar_tensor_tensor(out=q_dt[:], in0=q_dt[:], scalar=13.0 / 16.0, in1=e_dt[:],
                                         op0=ALU.add, op1=ALU.mult).then_inc(d_poly, 1)
                dve.wait_ge(d_ln, n + 1)
                dve.wait_ge(d_mask, n + 1)
                dve.wait_ge(d_poly, n + 1)
                dve.copy_predicated(q_dt[:], m_dt[:], l_dt[:]).then_inc(d_sel, 1)
                dve.wait_ge(d_sel, n + 1)
                if not (isinstance(n, int) and n < 2):
                    dve.wait_ge(exp_done, (n - 1) * (2 * PAIRS))
                    dve.wait_ge(d_dtu, n - 1)
                dve.scalar_tensor_tensor(out=dt[:, k % 2, :], in0=work0[:], scalar=0.0, in1=q_dt[:],
                                         op0=ALU.max, op1=ALU.add).then_inc(d_dt, 1)

            def scan(s, j):
                dve.wait_ge(exp_done, (s * PAIRS + j) * 2 + 2)
                dve.wait_ge(mulb, s * PAIRS + j + 1)
                if not (isinstance(s, int) and s * PAIRS + j < H_RING):
                    dve.wait_ge(summed, s * PAIRS + j + 1 - H_RING)
                dve.tensor_tensor_scan(h[:, j % H_RING].rearrange("p i l -> p (i l)"),
                                       dA[:, j % 2].rearrange("p i l -> p (i l)"),
                                       dbu[:, j % 2].rearrange("p i l -> p (i l)"), 0.0, ALU.mult, ALU.add
                                       ).then_inc(scanned, 1)

            def times_c(b, s, j):
                dve.wait_ge(scanned, s * PAIRS + j + 1)
                dve.wait_ge(c_landed[j], (b + 1) * 16)
                dve.tensor_tensor(h[:, j % H_RING], h[:, j % H_RING], c_rep[:, j], ALU.mult).then_inc(mulc, 1)

            def gate_y(s, k):
                dve.wait_ge(summed, (s + 1) * PAIRS)
                dve.wait_ge(g_done, s + 1)
                if not (isinstance(s, int) and s == 0):
                    dve.wait_ge(y_turned, s)
                dve.tensor_tensor(yg[:], y[k % 2][:], gate[:, k, :], ALU.mult).then_inc(gated, 1)

            def add_x1(b, k, s):
                dve.wait_ge(y_turned, s + 1)
                dve.wait_ge(g_zn, (b + 1) * KB)
                dve.tensor_tensor(x1_columns(b, k), work1[:].rearrange("p (t d) -> p t d", t=KB),
                                  x1_columns(b, k), ALU.add).then_inc(x1_added, 1)

            def t_stats(b, k, t):
                dve.wait_ge(x1_added, (b + 1) * KB)
                if not (isinstance(t, int) and t == 0):
                    dve.wait_ge(t_xn, t)
                dve.bn_stats(t_stat[:], x1_block(b, k)).then_inc(t_bn, 1)
                dve.wait_ge(t_bn, t + 1)
                dve.bn_aggr(t_mv[:], t_stat[:]).then_inc(t_aggr, 1)

            def t_refine(t):
                dve.wait_ge(t_expv, t + 1)
                refine(t_r, t_mv, t_newton, t)

            def t_final_(b, k, t):
                dve.wait_ge(t_ffn, t + 1)
                dve.tensor_tensor(x1_block(b, k), work1[:], x1_block(b, k), ALU.add).then_inc(t_final, 1)

            def step(b, k, first, last):
                s = b * KB + k
                ng = s + KB - 1
                kg = (k + KB - 1) % KB
                bg = b if k == 0 else b + 1
                gates = not last or k == 0
                kp, bp = (k - 1) % KB, (b if k else b - 1)
                for j in range(PAIRS):
                    if j == 0 and gates:
                        if k == 1:
                            dve.wait_ge(x_landed, (b + 2) * 16)
                        g_stats(bg, kg, ng)
                    if j == 1:
                        if not (first and k == 0):
                            gate_y(s - 1, kp)
                        if not last:
                            conv_rest(work0, s + KB, k)
                    if j == 2:
                        if not (first and k == 0):
                            add_x1(bp, kp, s - 1)
                        if gates:
                            g_refine(ng)
                    if j == 3 and not first:
                        t_stats(b - 1, k, s - KB)
                    if j == 4:
                        if not last:
                            u_arg_(s + KB, k)
                        if not first:
                            t_refine(s - KB)
                    if j == 7:
                        if k < KB - 1:
                            softplus(s + 1, k + 1)
                        if gates:
                            g_arg_(ng, kg)
                    scan(s, j)
                    if j > 0:
                        times_c(b, s, j - 1)
                times_c(b, s, PAIRS - 1)
                if k == KB - 1 and not last:
                    softplus(s + 1, 0)
                if not first:
                    t_final_(b - 1, k, s - KB)

            dve.memset(eps_col, EPS)
            dve.memset(sq_col, -0.75 * SQ_SCALE)
            dve.memset(w_dt[:], 0.0)
            dve.memset(w_x[:, :, 2 * N + BC_ROW:P], 0.0)
            dve.memset(bias_row[:], 0.0)
            dve.memset(ones_row[:], 1.0)
            dve.memset(dt_low[:], 1.0).then_inc(pads_ready, 1)
            dve.memset(dA[:, :, :, 0:1], 0.0).then_inc(da_zero, 1)
            banks = [work0, work1, y[0], y[1]]
            for k in range(KB):
                conv_rest(banks[k], k, k)
                u_arg_(k, k)
            dve.wait_ge(ident_ready, 1)
            dve.wait_ge(ch_landed, 16)
            for k in range(KB):
                dve.tensor_scalar(diag_d[:, k, :], ident[:], dsk[:, k:k + 1], None, ALU.mult).then_inc(diag_ready, 1)
            softplus(0, 0)
            dve.wait_ge(x_landed, 16)
            for k in range(KB - 1):
                g_stats(0, k, k)
                g_refine(k)
                g_arg_(k, k)
            for b in range(BATCH):
                for k in range(KB):
                    step(b, k, b == 0, b == BATCH - 1)
            gate_y(STEPS - 1, KB - 1)
            add_x1(BATCH - 1, KB - 1, STEPS - 1)
            for k in range(KB):
                t = STEPS - KB + k
                t_stats(BATCH - 1, k, t)
                t_refine(t)
                t_final_(BATCH - 1, k, t)

        @block.gpsimd
        def _(pool):
            def u_times(n, k):
                pool.wait_ge(u_sig, n + 1)
                pool.tensor_tensor(u[:, k, :], acc[:, k % 2, :], ut[:, k % 2, :], ALU.mult).then_inc(u_done, 1)

            def g_times(n, k):
                pool.wait_ge(g_sig, n + 1)
                pool.tensor_tensor(gate[:, k, :], gate[:, k, :], gt[:, k % 2, :], ALU.mult).then_inc(g_done, 1)

            def dt_times_u(n, k):
                pool.wait_ge(d_dt, n + 1)
                pool.wait_ge(u_done, n + 1)
                pool.tensor_tensor(dtu[:, k % 2, :], dt[:, k % 2, :], u[:, k, :], ALU.mult).then_inc(d_dtu, 1)

            def times_b(b, s, k, j):
                pool.wait_ge(b_landed[j], (b + 1) * 16)
                if not (isinstance(s, int) and s * PAIRS + j < 2):
                    pool.wait_ge(scanned, s * PAIRS + j - 1)
                pool.tensor_tensor(dbu[:, j % 2], b_rep[:, j],
                                   dtu[:, k % 2, :].unsqueeze(1).to_broadcast([P, 2, L]), ALU.mult).then_inc(mulb, 1)

            def load_factor(r):
                src = factors[r].rearrange("(k p) e -> p k e", p=P)
                if r == 0:
                    pool.dma_start(fsum[:], src).then_inc(f_landed, 16)
                else:
                    pool.wait_ge(f_landed, r * 16)
                    pool.dma_start(fsum[:], src, accum_op=ALU.add).then_inc(f_landed, 16)

            def step(b, k, first, last):
                s = b * KB + k
                pool.wait_ge(d_dtu, s + 1)
                for j in range(PAIRS):
                    if j == 5 and not last:
                        pool.wait_ge(y_init, s + 1)
                        u_times(s + KB, k)
                    if first and k == 0:
                        load_factor(j)
                    times_b(b, s, k, j)
                if not (last and k == KB - 1):
                    dt_times_u(s + 1, (k + 1) % KB)
                if not last or k == 0:
                    g_times(s + KB - 1, (k + KB - 1) % KB)

            pool.memset(ident[:], 0.0).then_inc(ident_zero, 1)
            pool.wait_ge(ident_zero, 1)
            pool.affine_select(out=ident[:], in_=ident[:], compare_op=ALU.not_equal, fill=1.0, base=0,
                               pattern=[[-1, P]], channel_multiplier=1).then_inc(ident_ready, 1)
            for k in range(KB):
                u_times(k, k)
            dt_times_u(0, 0)
            for k in range(KB - 1):
                g_times(k, k)
            for b in range(BATCH):
                for k in range(KB):
                    step(b, k, b == 0, b == BATCH - 1)


def kernel(**inputs):
    import numpy as np
    import concourse.bacc as bacc
    from concourse.bass_utils import run_bass_kernel_spmd

    a = {n: np.asarray(v) for n, v in inputs.items()}
    f32 = np.float32
    xp = np.zeros((DI, BC_ROW + 2 * N), f32)
    xp[:, 0:RANK] = a["L0_xattn_x_proj_w"].T[:, 0:RANK]
    xp[:, BC_ROW:] = a["L0_xattn_x_proj_w"].T[:, RANK:]
    arrays = {
        "x": a["x"],
        "ctxT": a["ctx_1024"].transpose(2, 0, 1),
        "w_inT": a["L0_xattn_in_proj_w"].T,
        "channel": np.concatenate([a["L0_xattn_conv_w"].reshape(DI, TAPS), a["L0_xattn_conv_b"][:, None],
                                   a["L0_xattn_D"][:, None], a["L0_xattn_A_log"]], axis=1),
        "x_projT": xp,
        "dt_wT": np.concatenate([a["L0_xattn_dt_proj_w"].T, a["L0_xattn_dt_proj_b"][None]]),
        "factors": a["L0_ffn_factors"],
        "bias": a["L0_ffn_bias"].reshape(1, DI),
    }
    arrays = {n: np.ascontiguousarray(v) for n, v in arrays.items()}
    nc = bacc.Bacc("TRN2", target_bir_lowering=False, num_devices=1)
    args = [nc.dram_tensor(n, v.shape, mybir.dt.from_np(v.dtype), kind="ExternalInput").ap()
            for n, v in arrays.items()]
    out = nc.dram_tensor("out", (BATCH, L, DI), F32, kind="ExternalOutput").ap()
    build(nc, *args, out)
    r = run_bass_kernel_spmd(nc, [arrays], core_ids=[0])
    return r.results[0]["out"]
```

```python
from contextlib import ExitStack

import concourse.bass as bass
from concourse import mybir

ALU = mybir.AluOpType
ACT = mybir.ActivationFunctionType
F32 = mybir.dt.float32
U32 = mybir.dt.uint32

P = 128
BATCH, L, DM = 4, 512, 256
DI, N, TAPS, RANK = 512, 16, 4, 16
KB = DI // P
CB = DM // P
FR = 8
PAIRS = N // 2
STEPS = BATCH * KB
EPS = 1e-5
H_RING = 4
BC_ROW = 32
POLY_BELOW = 2.0 ** -7
SQ_SCALE = 3.0 ** -0.5


def build(nc, x, ctxT, w_inT, channel, x_projT, dt_wT, factors, bias, out):
    bc_dram = nc.dram_tensor("bc_scratch", (BATCH, 2 * N, L), F32, kind="Internal").ap()

    with ExitStack() as ctx:
        def sb(name, shape, dt=F32):
            return ctx.enter_context(nc.sbuf_tensor(name, shape, dt))

        def ps(name, shape):
            return ctx.enter_context(nc.psum_tensor(name, shape, F32))

        def sem(name):
            return ctx.enter_context(nc.semaphore(name))

        ident = sb("ident", [P, P])
        diag_d = sb("diag_d", [P, KB, P])
        ones_row = sb("ones_row", [P, P])
        bias_row = sb("bias_row", [P, DI])
        w_in = sb("w_in", [P, CB, DI])
        chan = sb("chan", [P, KB, TAPS + 2 + N])
        cw = chan[:, :, 0:TAPS]
        cb = chan[:, :, TAPS]
        dsk = chan[:, :, TAPS + 1]
        a_log = chan[:, :, TAPS + 2:]
        w_x = sb("w_x", [P, KB, 2 * N + BC_ROW])
        w_dt = sb("w_dt", [P, DI])
        a_neg = sb("a_neg", [P, KB, N])
        fsum = sb("fsum", [P, KB, DI])
        ctx_sb = sb("ctx_sb", [P, CB, L])
        x1 = sb("x1", [P, BATCH * KB * DI])
        b_rep = sb("b_rep", [P, PAIRS, 2, L])
        c_rep = sb("c_rep", [P, PAIRS, 2, L])
        bc = sb("bc", [2 * N + BC_ROW, L])
        dt_low = sb("dt_low", [P, L])
        u = sb("u", [P, 2, KB, L])
        acc = sb("acc", [P, 2, L])
        ut = sb("ut", [P, 2, L])
        gate = sb("gate", [P, KB, L])
        ur = sb("ur", [P, L])
        gt = sb("gt", [P, 2, L])
        g_stat = sb("g_stat", [P, KB, 6])
        g_mv = sb("g_mv", [P, KB, 2])
        g_r = sb("g_r", [P, 3, KB])
        e_dt = sb("e_dt", [P, L])
        l_dt = sb("l_dt", [P, L])
        q_dt = sb("q_dt", [P, L])
        m_dt = sb("m_dt", [P, L], mybir.dt.uint8)
        dt = sb("dt", [P, 2, L])
        dtu = sb("dtu", [P, 2, L])
        dbu = sb("dbu", [P, 2, 2, L])
        h = sb("h", [P, H_RING, 2, L])
        yg = sb("yg", [P, L])
        xn = sb("xn", [P, DI])
        xnT = sb("xnT", [P, KB, P])
        t_stat = sb("t_stat", [P, KB, 6])
        t_mv = sb("t_mv", [P, KB, 2])
        t_r = sb("t_r", [P, 3, KB])
        cols = sb("cols", [P, 2])
        eps_col, sq_col = cols[:, 0:1], cols[:, 1:2]

        dA = ps("dA", [P, 2, 2, L])
        y = ps("y", [P, L])
        work0 = ps("work0", [P, L])
        work1 = ps("work1", [P, L])
        work2 = ps("work2", [P, L])

        w_in_landed, w_x_landed, w_dt_landed, bias_landed, ch_landed = (
            sem(f"{n}_landed") for n in ("w_in", "w_x", "w_dt", "bias", "ch"))
        ctx_landed = sem("ctx_landed")
        x_landed = sem("x_landed")
        ident_zero = sem("ident_zero")
        ident_ready = sem("ident_ready")
        pads_ready = sem("pads_ready")
        da_zero = sem("da_zero")
        diag_ready = sem("diag_ready")
        a_exp = sem("a_exp")
        a_ready = sem("a_ready")
        f_landed = sem("f_landed")
        f_scaled = sem("f_scaled")
        in_mm = sem("in_mm")
        tap = sem("tap")
        conv = sem("conv")
        u_abs, u_exp, u_relu, u_ln, u_arg, u_sig, u_done = (
            sem(f"u_{n}") for n in ("abs", "exp", "relu", "ln", "arg", "sig", "done"))
        g_bn, g_aggr, g_lnv, g_expv, g_nb, g_zn, g_exp, g_ln, g_sig, g_done = (
            sem(f"g_{n}") for n in ("bn", "aggr", "lnv", "expv", "nb", "zn", "exp", "ln", "sig", "done"))
        f_bn, f_aggr, f_lnv, f_expv, f_nb, f_zn, f_exp, f_ln, f_sig, f_done = (
            sem(f"f_{n}") for n in ("bn", "aggr", "lnv", "expv", "nb", "zn", "exp", "ln", "sig", "done"))
        x_mm = sem("x_mm")
        bc_evac = sem("bc_evac")
        dtl_evac = sem("dtl_evac")
        bc_stored = sem("bc_stored")
        b_landed = [sem(f"b_landed{j}") for j in range(PAIRS)]
        c_landed = [sem(f"c_landed{j}") for j in range(PAIRS)]
        d_mm, d_abs, d_exp, d_ln, d_sq, d_poly, d_mask, d_sel, d_dt, d_dtu = (
            sem(f"d_{n}") for n in ("mm", "abs", "exp", "ln", "sq", "poly", "mask", "sel", "dt", "dtu"))
        y_init = sem("y_init")
        exp_done = sem("exp_done")
        mulb = sem("mulb")
        scanned = sem("scanned")
        mulc = sem("mulc")
        summed = sem("summed")
        gated = sem("gated")
        y_turned = sem("y_turned")
        x1_added = sem("x1_added")
        t_bn, t_aggr, t_lnv, t_expv, t_nb, t_xn, t_turned, t_xnT, t_ffn, t_final = (
            sem(f"t_{n}") for n in ("bn", "aggr", "lnv", "expv", "nb", "xn", "turned", "xnT", "ffn", "final"))
        z_bn, z_aggr, z_lnv, z_expv, z_nb, z_xn, z_turned, z_xnT, z_ffn, z_final = (
            sem(f"z_{n}") for n in ("bn", "aggr", "lnv", "expv", "nb", "xn", "turned", "xnT", "ffn", "final"))
        out_stored = sem("out_stored")

        def x1_block(b, k):
            return x1[:, bass.ds(b * (KB * DI) + k * DI, DI)]

        acc_of = lambda n: h[:, n, 0, :] if n < KB else acc[:, n % 2, :]
        ut_of = lambda n: h[:, n, 1, :] if n < KB else ut[:, n % 2, :]
        first_banks = [work0, work1, work2, y]
        z_turn_bank = [dA[:, i // 2, i % 2, :] for i in range(KB)]
        z_ffn_bank = [work2, work0, work1, y]
        first_gates = gate[:, 0:KB - 1, :].rearrange("p k l -> p (k l)")
        first_gt = x1[:, (BATCH - 1) * KB * DI:(BATCH * KB - 1) * DI]

        def x1_columns(b, k):
            return x1[:, bass.ds(b * (KB * DI), KB * DI)].rearrange("p (t d) -> p t d", t=KB)[:, :, k * P:(k + 1) * P]

        block = ctx.enter_context(nc.Block())

        @block.sync
        def _(sp):
            sp.dma_start(ctx_sb[:], ctxT[:, 0, :].rearrange("(c p) l -> p c l", p=P)).then_inc(ctx_landed, 16)
            sp.dma_start(w_in[:], w_inT.rearrange("(c p) e -> p c e", p=P)).then_inc(w_in_landed, 16)
            sp.dma_start(chan[:], channel.rearrange("(k p) t -> p k t", p=P)).then_inc(ch_landed, 16)
            sp.dma_start(w_x[:], x_projT.rearrange("(k p) e -> p k e", p=P)).then_inc(w_x_landed, 16)
            sp.wait_ge(pads_ready, 1)
            sp.dma_start(w_dt[0:RANK + 1, :], dt_wT).then_inc(w_dt_landed, 16)
            sp.dma_start(bias_row[0:1, :], bias).then_inc(bias_landed, 16)
            sp.dma_start(x1[:, 0:KB * DI].rearrange("p (t d) -> p t d", t=KB),
                         x[0].rearrange("(t p) d -> p t d", p=P)).then_inc(x_landed, 16)
            sp.wait_ge(in_mm, KB)
            sp.wait_ge(ctx_landed, 16)
            sp.dma_start(ctx_sb[:], ctxT[:, 1, :].rearrange("(c p) l -> p c l", p=P)).then_inc(ctx_landed, 16)

            def spread_bc(b):
                sp.wait_ge(bc_evac, b + 1)
                sp.dma_start(bc_dram[bass.ds(b, 1)].rearrange("b n l -> (b n) l"),
                             bc[BC_ROW:BC_ROW + 2 * N, :]).then_inc(bc_stored, 16)
                sp.wait_ge(bc_stored, (b + 1) * 16)
                rows = bc_dram[bass.ds(b, 1)].rearrange("b n l -> b (n l)")
                for j in range(PAIRS):
                    if b > 0:
                        sp.wait_ge(mulb, b * (KB * PAIRS) - PAIRS + j + 1)
                    sp.dma_start(b_rep[:, j].rearrange("p i l -> p (i l)"),
                                 rows[:, 2 * j * L:(2 * j + 2) * L].to_broadcast([P, 2 * L])).then_inc(b_landed[j], 16)
                    if b > 0:
                        sp.wait_ge(mulc, b * (KB * PAIRS) - PAIRS + j + 1)
                    sp.dma_start(c_rep[:, j].rearrange("p i l -> p (i l)"),
                                 rows[:, (N + 2 * j) * L:(N + 2 * j + 2) * L].to_broadcast([P, 2 * L])
                                 ).then_inc(c_landed[j], 16)

            def store(b, k):
                if b < BATCH - 1:
                    sp.wait_ge(t_final, b * KB + k + 1)
                else:
                    sp.wait_ge(z_final, k + 1)
                sp.dma_start(out[bass.ds(b, 1), k * P:(k + 1) * P, :].rearrange("b p d -> (b p) d"),
                             x1_block(b, k)).then_inc(out_stored, 16)

            spread_bc(0)
            for b in range(BATCH):
                if b + 1 < BATCH:
                    sp.wait_ge(x_landed, (b + 1) * 16)
                    if b + 2 == BATCH:
                        sp.wait_ge(f_done, 1)
                    sp.dma_start(x1[:, (b + 1) * KB * DI:(b + 2) * KB * DI].rearrange("p (t d) -> p t d", t=KB),
                                 x[b + 1].rearrange("(t p) d -> p t d", p=P)).then_inc(x_landed, 16)
                if b >= 2:
                    store(b - 2, KB - 1)
                if b >= 1:
                    store(b - 1, 0)
                if b + 2 < BATCH:
                    sp.wait_ge(in_mm, (b + 2) * KB)
                    sp.wait_ge(ctx_landed, (b + 2) * 16)
                    sp.dma_start(ctx_sb[:], ctxT[:, b + 2, :].rearrange("(c p) l -> p c l", p=P)
                                 ).then_inc(ctx_landed, 16)
                if b >= 1:
                    store(b - 1, 1)
                if b + 1 < BATCH:
                    spread_bc(b + 1)
                if b >= 1:
                    store(b - 1, 2)
            store(BATCH - 2, KB - 1)
            for k in range(KB):
                store(BATCH - 1, k)
            sp.wait_ge(out_stored, STEPS * 16)

        @block.tensor
        def _(pe):
            def in_proj(bank, k):
                for c in range(CB):
                    mm = pe.matmul(bank[:], w_in[:, c, k * P:(k + 1) * P], ctx_sb[:, c, :],
                                   start=(c == 0), stop=(c == CB - 1))
                mm.then_inc(in_mm, 1)

            def x_proj(ub, ks):
                for k in ks:
                    mm = pe.matmul(work2[0:2 * N + BC_ROW, :], w_x[:, k, :], u[:, ub % 2, k, :], start=(k == 0),
                                   stop=(k == KB - 1))
                if KB - 1 in ks:
                    mm.then_inc(x_mm, 1)

            def dt_proj(k):
                pe.matmul(work2[:], w_dt[:, k * P:(k + 1) * P], dt_low[:], start=True, stop=True).then_inc(d_mm, 1)

            def turn_y(s):
                pe.wait_ge(gated, s + 1)
                for t in range(KB):
                    tr = pe.transpose(work0[:, t * P:(t + 1) * P], yg[:, t * P:(t + 1) * P], ident[:])
                tr.then_inc(y_turned, 1)

            def turn_xn(t):
                pe.wait_ge(t_xn, t + 1)
                for k in range(KB):
                    tr = pe.transpose(work1[:, k * P:(k + 1) * P], xn[:, k * P:(k + 1) * P], ident[:])
                tr.then_inc(t_turned, 1)

            def last_layer(t, half):
                if half == 0:
                    pe.wait_ge(t_xnT, t + 1)
                for k in (0, 1) if half == 0 else (2, 3):
                    pe.matmul(work1[:], xnT[:, k, :], fsum[:, k, :], start=(k == 0), stop=False)
                if half == 1:
                    pe.matmul(work1[:], ones_row[:], bias_row[:], start=False, stop=True).then_inc(t_ffn, 1)

            def state_sum(s, j):
                pe.wait_ge(mulc, s * PAIRS + j + 1)
                for i in range(2):
                    mm = pe.matmul(y[:], ident[:], h[:, j % H_RING, i, :], start=False,
                                   stop=(j == PAIRS - 1 and i == 1))
                mm.then_inc(summed, 1)

            def step(s):
                b, k = divmod(s, KB)
                nu, nt = s + KB + 2, s - KB
                turns = k == KB - 1 and b + 1 < BATCH
                if turns:
                    pe.wait_ge(u_done, s + KB - 2)
                    pe.wait_ge(d_dt, s + 1)
                    x_proj(b + 1, (0, 1))
                    pe.wait_ge(u_done, s + KB + 1)
                    x_proj(b + 1, (2, 3))
                elif s + 1 < STEPS:
                    pe.wait_ge(d_dt, s + 1)
                    dt_proj(k + 1)
                pe.wait_ge(u_done, s + 1)
                if s > 0:
                    pe.wait_ge(gated, s)
                pe.matmul(y[:], diag_d[:, k, :], u[:, b % 2, k, :], start=True, stop=False).then_inc(y_init, 1)
                if s > 0:
                    pe.wait_ge(conv, min(s + KB + 2, STEPS) * 3)
                    turn_y(s - 1)
                for j in range(PAIRS):
                    state_sum(s, j)
                    if j == 1:
                        if turns:
                            pe.wait_ge(bc_evac, b + 2)
                            pe.wait_ge(dtl_evac, b + 2)
                            dt_proj(0)
                        if nt >= 1:
                            last_layer(nt - 1, 0)
                    if j == 3 and nu < STEPS:
                        pe.wait_ge(ctx_landed, (nu // KB + 1) * 16)
                        if s > 0:
                            pe.wait_ge(x1_added, s)
                        else:
                            pe.wait_ge(conv, KB * 3 + 3)
                        in_proj(work0, nu % KB)
                    if j == 4 and nt >= 1:
                        last_layer(nt - 1, 1)
                if nt >= 0:
                    if nt >= 1:
                        pe.wait_ge(t_final, nt)
                    turn_xn(nt)

            pe.wait_ge(ctx_landed, 16)
            pe.wait_ge(w_in_landed, 16)
            for k in range(KB):
                in_proj(first_banks[k], k)
            pe.wait_ge(ctx_landed, 32)
            pe.wait_ge(conv, 6)
            in_proj(work0, 0)
            in_proj(work1, 1)
            pe.wait_ge(w_x_landed, 16)
            pe.wait_ge(pads_ready, 1)
            pe.wait_ge(conv, 9)
            for k in range(KB):
                pe.wait_ge(u_done, k + 1)
                x_proj(0, [k])
            pe.wait_ge(w_dt_landed, 16)
            pe.wait_ge(bc_evac, 1)
            pe.wait_ge(dtl_evac, 1)
            dt_proj(0)
            pe.wait_ge(ident_ready, 1)
            pe.wait_ge(diag_ready, KB)
            pe.wait_ge(conv, 3 * KB)
            for s in range(STEPS):
                if s == KB + 1:
                    pe.wait_ge(f_scaled, 1)
                    pe.wait_ge(bias_landed, 16)
                step(s)
            last_layer(STEPS - KB - 1, 0)
            last_layer(STEPS - KB - 1, 1)
            turn_y(STEPS - 1)
            pe.wait_ge(scanned, STEPS * PAIRS)
            for i in range(KB):
                pe.wait_ge(z_xn, i + 1)
                for k in range(KB):
                    tr = pe.transpose(z_turn_bank[i][:, k * P:(k + 1) * P], h[:, i, 0, k * P:(k + 1) * P], ident[:])
                tr.then_inc(z_turned, 1)
            pe.wait_ge(x1_added, STEPS)
            pe.wait_ge(t_final, STEPS - KB)
            for i in range(KB):
                pe.wait_ge(z_xnT, i + 1)
                for k in range(KB):
                    pe.matmul(z_ffn_bank[i][:], h[:, i, 1, k * P:(k + 1) * P], fsum[:, k, :], start=(k == 0), stop=False)
                pe.matmul(z_ffn_bank[i][:], ones_row[:], bias_row[:], start=False, stop=True).then_inc(z_ffn, 1)

        @block.scalar
        def _(act):
            def conv_tap(bank, n, k):
                act.wait_ge(in_mm, n + 1)
                if n >= KB + 2:
                    act.wait_ge(u_done, n - 1)
                act.activation(acc_of(n), bank[:], ACT.Identity, bias=cb[:, k:k + 1],
                               scale=cw[:, k, TAPS - 1:TAPS]).then_inc(tap, 1)

            def u_abs_(n):
                act.wait_ge(conv, n * 3 + 3)
                act.activation(ut_of(n), acc_of(n), ACT.Abs).then_inc(u_abs, 1)

            def u_exp_(n):
                act.wait_ge(u_abs, n + 1)
                act.activation(ut_of(n), ut_of(n), ACT.Exp, scale=-1.0).then_inc(u_exp, 1)

            def u_relu_(n):
                if n > 0:
                    act.wait_ge(u_arg, n)
                act.activation(ur[:], acc_of(n), ACT.Relu, scale=-1.0).then_inc(u_relu, 1)

            def u_ln_(n):
                act.wait_ge(u_exp, n + 1)
                act.activation(ut_of(n), ut_of(n), ACT.Ln, bias=1.0).then_inc(u_ln, 1)

            def u_sig_(n):
                act.wait_ge(u_arg, n + 1)
                act.activation(ut_of(n), ut_of(n), ACT.Exp, scale=-1.0).then_inc(u_sig, 1)

            def lnv(r, mv, ks, after, n, done):
                act.wait_ge(after, n)
                act.activation(r[:, 0, ks], mv[:, ks, 1], ACT.Ln, bias=eps_col).then_inc(done, 1)

            def expv(r, ks, after, n, done):
                act.wait_ge(after, n)
                act.activation(r[:, 1, ks], r[:, 0, ks], ACT.Exp, scale=-0.5).then_inc(done, 1)

            def norm(dst, b, k, r, done):
                act.activation(dst, x1_block(b, k), ACT.Identity, bias=r[:, 2, k:k + 1],
                               scale=r[:, 1, k:k + 1]).then_inc(done, 1)

            def g_zn_(n):
                if n >= KB:
                    act.wait_ge(gated, n - KB + 1)
                act.wait_ge(g_nb, n - 2)
                norm(gate[:, n % KB, :], n // KB, n % KB, g_r, g_zn)

            def g_exp_(n):
                act.wait_ge(g_zn, n - 2)
                if n >= 5:
                    act.wait_ge(g_done, n - 4)
                act.activation(gt[:, n % 2, :], gate[:, n % KB, :], ACT.Exp, scale=-1.0).then_inc(g_exp, 1)

            def g_ln_(n):
                act.wait_ge(g_exp, n - 2)
                act.activation(gt[:, n % 2, :], gt[:, n % 2, :], ACT.Ln, bias=1.0).then_inc(g_ln, 1)

            def g_sig_(n):
                act.wait_ge(g_ln, n - 2)
                act.activation(gt[:, n % 2, :], gt[:, n % 2, :], ACT.Exp, scale=-1.0).then_inc(g_sig, 1)

            def x_evac(b):
                act.wait_ge(x_mm, b + 1)
                if b > 0:
                    act.wait_ge(bc_stored, b * 16)
                    act.wait_ge(d_mm, b * KB)
                act.activation(bc[BC_ROW:BC_ROW + 2 * N, :], work2[BC_ROW:BC_ROW + 2 * N, :], ACT.Copy
                               ).then_inc(bc_evac, 1)
                act.activation(dt_low[0:RANK, :], work2[0:RANK, :], ACT.Copy).then_inc(dtl_evac, 1)

            def d_abs_(n):
                act.wait_ge(d_mm, n + 1)
                if n > 0:
                    act.wait_ge(d_dt, n)
                act.activation(e_dt[:], work2[:], ACT.Abs).then_inc(d_abs, 1)

            def d_exp_(n):
                act.wait_ge(d_abs, n + 1)
                act.activation(e_dt[:], e_dt[:], ACT.Exp, scale=-1.0).then_inc(d_exp, 1)

            def d_ln_(n):
                act.wait_ge(d_exp, n + 1)
                act.activation(l_dt[:], e_dt[:], ACT.Ln, bias=1.0).then_inc(d_ln, 1)

            def d_sq_(n):
                act.activation(q_dt[:], e_dt[:], ACT.Square, scale=SQ_SCALE, bias=sq_col).then_inc(d_sq, 1)

            def t_xn_(t):
                act.wait_ge(t_nb, t + 1)
                if t > 0:
                    act.wait_ge(t_turned, t)
                norm(xn[:], t // KB, t % KB, t_r, t_xn)

            def t_xnT_(t):
                act.wait_ge(t_turned, t + 1)
                if t > 0:
                    act.wait_ge(t_ffn, t)
                act.activation(xnT[:].rearrange("p k l -> p (k l)"), work1[:], ACT.Copy).then_inc(t_xnT, 1)

            def decay(s, k, j, i):
                act.activation(dA[:, j % 2, i, 1:L], dt[:, k % 2, 1:L], ACT.Exp,
                               scale=a_neg[:, k, 2 * j + i:2 * j + i + 1]).then_inc(exp_done, 1)

            def step(s):
                b, k = divmod(s, KB)
                nu, ng, nt = s + KB + 1, s + KB - 1, s - KB
                is_u, is_g, is_t, is_d = nu < STEPS, ng < STEPS, nt >= 0, s + 1 < STEPS
                for j in range(PAIRS):
                    if j == 2:
                        if s == 0:
                            u_sig_(KB)
                        if is_u:
                            u_abs_(nu)
                    if j == 3:
                        if k == KB - 1 and is_d:
                            x_evac(b + 1)
                        if is_u:
                            u_relu_(nu)
                            u_ln_(nu)
                    if j == 5 and is_g:
                        expv(g_r, slice(ng % KB, ng % KB + 1), g_lnv, ng - 2, g_expv)
                    if j == 5 and is_d:
                        d_abs_(s + 1)
                    if j == 6:
                        if is_u:
                            u_sig_(nu)
                        if is_d:
                            d_ln_(s + 1)
                            d_sq_(s + 1)
                    if j == 7 and is_g:
                        g_zn_(ng)
                    if s * PAIRS + j >= 2:
                        act.wait_ge(scanned, s * PAIRS + j - 1)
                    decay(s, k, j, 0)
                    if j == 2:
                        if is_u:
                            u_exp_(nu)
                        if nt >= 1:
                            t_xnT_(nt - 1)
                    if j == 4 and is_g:
                        lnv(g_r, g_mv, slice(ng % KB, ng % KB + 1), g_aggr, ng - 2, g_lnv)
                    if j == 5:
                        if is_d:
                            d_exp_(s + 1)
                        if is_t:
                            lnv(t_r, t_mv, slice(k, k + 1), t_aggr, nt + 1, t_lnv)
                    if j == 6 and is_t:
                        expv(t_r, slice(k, k + 1), t_lnv, nt + 1, t_expv)
                    if j == 7:
                        if nu + 1 < STEPS:
                            conv_tap(work0, nu + 1, (nu + 1) % KB)
                        if is_g:
                            g_exp_(ng)
                    decay(s, k, j, 1)
                    if s == 0 and j == 1:
                        act.wait_ge(f_zn, 3)
                        act.activation(first_gt, first_gates, ACT.Exp, scale=-1.0).then_inc(f_exp, 1)
                    if s == 0 and j == 3:
                        act.wait_ge(f_exp, 1)
                        act.activation(first_gt, first_gt, ACT.Ln, bias=1.0).then_inc(f_ln, 1)
                    if s == 0 and j == 5:
                        act.wait_ge(f_ln, 1)
                        act.activation(first_gt, first_gt, ACT.Exp, scale=-1.0).then_inc(f_sig, 1)
                    if j == 6 and s == KB:
                        act.wait_ge(f_landed, FR * 16)
                        act.activation(fsum[:], fsum[:], ACT.Copy, scale=FR ** -0.5).then_inc(f_scaled, 1)
                if is_g:
                    g_ln_(ng)
                    g_sig_(ng)
                if is_t:
                    t_xn_(nt)

            act.preload_act_table_set("natural_log_exp_and_others")
            act.wait_ge(ch_landed, 16)
            act.wait_ge(pads_ready, 1)
            act.activation(a_neg[:], a_log, ACT.Exp).then_inc(a_exp, 1)
            act.wait_ge(a_exp, 1)
            act.activation(a_neg[:], a_neg[:], ACT.Copy, scale=-1.0).then_inc(a_ready, 1)
            for k in range(KB):
                conv_tap(first_banks[k], k, k)
                if k == 1:
                    u_abs_(0)
                    u_exp_(0)
                    u_relu_(0)
                    u_ln_(0)
            for k in range(1, KB):
                u_abs_(k)
                u_exp_(k)
                u_relu_(k)
                u_ln_(k)
                u_sig_(k - 1)
            conv_tap(work0, KB, 0)
            conv_tap(work1, KB + 1, 1)
            u_sig_(KB - 1)
            x_evac(0)
            d_abs_(0)
            d_exp_(0)
            d_ln_(0)
            d_sq_(0)
            lnv(g_r, g_mv, slice(0, 3), f_aggr, 3, f_lnv)
            expv(g_r, slice(0, 3), f_lnv, 1, f_expv)
            u_abs_(KB)
            u_exp_(KB)
            u_relu_(KB)
            u_ln_(KB)
            act.wait_ge(f_nb, 1)
            for k in range(KB - 1):
                norm(gate[:, k, :], 0, k, g_r, f_zn)
            act.wait_ge(a_ready, 1)
            act.wait_ge(da_zero, 1)
            for s in range(STEPS):
                act.wait_ge(d_dt, s + 1)
                step(s)
            t_xnT_(STEPS - KB - 1)
            lnv(t_r, t_mv, slice(0, KB), z_aggr, KB, z_lnv)
            expv(t_r, slice(0, KB), z_lnv, 1, z_expv)
            act.wait_ge(z_nb, 1)
            act.wait_ge(summed, STEPS * PAIRS)
            for i in range(KB):
                norm(h[:, i, 0, :], BATCH - 1, i, t_r, z_xn)

        @block.vector
        def _(dve):
            def conv_part(bank, n, k, i):
                if i == 1:
                    dve.wait_ge(tap, n + 1)
                else:
                    dve.wait_ge(conv, n * 3 + i - 1)
                dve.scalar_tensor_tensor(out=acc_of(n)[:, i:L], in0=bank[:, 0:L - i],
                                         scalar=cw[:, k, TAPS - 1 - i:TAPS - i], in1=acc_of(n)[:, i:L],
                                         op0=ALU.mult, op1=ALU.add).then_inc(conv, 1)

            def stats(stat, b, k, done):
                dve.bn_stats(stat[:, k, :], x1_block(b, k)).then_inc(done, 1)

            def aggr(mv, stat, k, after, n, done):
                dve.wait_ge(after, n)
                dve.bn_aggr(mv[:, k, :], stat[:, k, :]).then_inc(done, 1)

            def shift(r, mv, ks, after, n, done):
                dve.wait_ge(after, n)
                dve.scalar_tensor_tensor(out=r[:, 2, ks], in0=mv[:, ks, 0], scalar=-1.0, in1=r[:, 1, ks],
                                         op0=ALU.mult, op1=ALU.mult).then_inc(done, 1)

            def softplus_parts(n):
                dve.wait_ge(d_exp, n + 1)
                dve.tensor_scalar(m_dt[:], e_dt[:], POLY_BELOW, None, ALU.is_ge).then_inc(d_mask, 1)
                dve.wait_ge(d_sq, n + 1)
                dve.scalar_tensor_tensor(out=q_dt[:], in0=q_dt[:], scalar=13.0 / 16.0, in1=e_dt[:],
                                         op0=ALU.add, op1=ALU.mult).then_inc(d_poly, 1)

            def softplus_select(n):
                dve.wait_ge(d_ln, n + 1)
                dve.wait_ge(d_mask, n + 1)
                dve.wait_ge(d_poly, n + 1)
                dve.copy_predicated(q_dt[:], m_dt[:], l_dt[:]).then_inc(d_sel, 1)

            def softplus_sum(n):
                dve.wait_ge(d_sel, n + 1)
                if n >= 2:
                    dve.wait_ge(exp_done, (n - 1) * (2 * PAIRS))
                    dve.wait_ge(d_dtu, n - 1)
                dve.scalar_tensor_tensor(out=dt[:, n % 2, :], in0=work2[:], scalar=0.0, in1=q_dt[:],
                                         op0=ALU.max, op1=ALU.add).then_inc(d_dt, 1)

            def scan(s, j):
                dve.wait_ge(exp_done, (s * PAIRS + j) * 2 + 2)
                dve.wait_ge(mulb, s * PAIRS + j + 1)
                if s * PAIRS + j >= H_RING:
                    dve.wait_ge(summed, s * PAIRS + j + 1 - H_RING)
                dve.tensor_tensor_scan(h[:, j % H_RING].rearrange("p i l -> p (i l)"),
                                       dA[:, j % 2].rearrange("p i l -> p (i l)"),
                                       dbu[:, j % 2].rearrange("p i l -> p (i l)"), 0.0, ALU.mult, ALU.add
                                       ).then_inc(scanned, 1)

            def times_c(b, s, j):
                dve.wait_ge(scanned, s * PAIRS + j + 1)
                dve.wait_ge(c_landed[j], (b + 1) * 16)
                dve.tensor_tensor(h[:, j % H_RING], h[:, j % H_RING], c_rep[:, j], ALU.mult).then_inc(mulc, 1)

            def gate_y(s):
                dve.wait_ge(summed, (s + 1) * PAIRS)
                if s < KB - 1:
                    dve.wait_ge(f_done, 1)
                else:
                    dve.wait_ge(g_done, s - KB + 2)
                if s > 0:
                    dve.wait_ge(y_turned, s)
                dve.tensor_tensor(yg[:], y[:], gate[:, s % KB, :], ALU.mult).then_inc(gated, 1)

            def add_x1(s):
                b, k = divmod(s, KB)
                dve.wait_ge(y_turned, s + 1)
                dve.wait_ge(g_zn, b * KB + 1)
                dve.tensor_tensor(x1_columns(b, k), work0[:].rearrange("p (t d) -> p t d", t=KB),
                                  x1_columns(b, k), ALU.add).then_inc(x1_added, 1)

            def t_final_(t):
                dve.wait_ge(t_ffn, t + 1)
                dve.tensor_tensor(x1_block(t // KB, t % KB), work1[:], x1_block(t // KB, t % KB), ALU.add
                                  ).then_inc(t_final, 1)

            def step(s):
                b, k = divmod(s, KB)
                nv, ng, nt = s + KB + 2, s + KB - 1, s - KB
                is_c, is_g, is_t, is_d = nv < STEPS, ng < STEPS, nt >= 0, s + 1 < STEPS
                gb, gk = divmod(ng, KB)
                for j in range(PAIRS):
                    if j == 3:
                        if is_g:
                            aggr(g_mv, g_stat, gk, g_bn, ng - 2, g_aggr)
                        if s > 0:
                            add_x1(s - 1)
                    if j == 4 and is_t:
                        aggr(t_mv, t_stat, k, t_bn, nt + 1, t_aggr)
                    if j == 5 and is_g:
                        shift(g_r, g_mv, slice(gk, gk + 1), g_expv, ng - 2, g_nb)
                    if j == 6 and is_d:
                        softplus_parts(s + 1)
                    if j == 7:
                        if is_d:
                            softplus_sum(s + 1)
                        if is_t:
                            shift(t_r, t_mv, slice(k, k + 1), t_expv, nt + 1, t_nb)
                    scan(s, j)
                    if j == 0 and s > 0 and nv - 1 < STEPS:
                        conv_part(work0, nv - 1, (nv - 1) % KB, 3)
                    if j == 1 and s > 0:
                        gate_y(s - 1)
                    if j == 2 and is_g:
                        dve.wait_ge(x_landed, (gb + 1) * 16)
                        stats(g_stat, gb, gk, g_bn)
                    if j == 3 and is_t:
                        dve.wait_ge(x1_added, (nt // KB + 1) * KB)
                        stats(t_stat, b - 1, k, t_bn)
                    if j == 6 and is_d:
                        softplus_select(s + 1)
                    if j == 7 and is_c:
                        conv_part(work0, nv, nv % KB, 1)
                    if j > 0:
                        times_c(b, s, j - 1)
                if is_c:
                    conv_part(work0, nv, nv % KB, 2)
                if nt >= 1:
                    t_final_(nt - 1)
                times_c(b, s, PAIRS - 1)

            dve.memset(eps_col, EPS)
            dve.memset(sq_col, -0.75 * SQ_SCALE)
            dve.memset(w_dt[:], 0.0)
            dve.memset(bias_row[:], 0.0)
            dve.memset(ones_row[:], 1.0)
            dve.memset(dt_low[:], 1.0).then_inc(pads_ready, 1)
            dve.memset(dA[:, :, :, 0:1], 0.0).then_inc(da_zero, 1)
            for k in range(KB):
                for i in range(1, TAPS):
                    conv_part(first_banks[k], k, k, i)
            dve.wait_ge(ident_ready, 1)
            dve.wait_ge(ch_landed, 16)
            for k in range(KB):
                dve.tensor_scalar(diag_d[:, k, :], ident[:], dsk[:, k:k + 1], None, ALU.mult).then_inc(diag_ready, 1)
            dve.wait_ge(x_landed, 16)
            for k in range(KB - 1):
                stats(g_stat, 0, k, f_bn)
            for k in range(KB - 1):
                aggr(g_mv, g_stat, k, f_bn, k + 1, f_aggr)
            for n in (KB, KB + 1):
                for i in range(1, TAPS):
                    conv_part(first_banks[n - KB], n, n - KB, i)
            softplus_parts(0)
            softplus_select(0)
            softplus_sum(0)
            shift(g_r, g_mv, slice(0, KB - 1), f_expv, 1, f_nb)
            for s in range(STEPS):
                step(s)
            gate_y(STEPS - 1)
            t_final_(STEPS - KB - 1)
            add_x1(STEPS - 1)
            dve.wait_ge(x1_added, STEPS)
            for i in range(KB):
                stats(t_stat, BATCH - 1, i, z_bn)
            for i in range(KB):
                aggr(t_mv, t_stat, i, z_bn, i + 1, z_aggr)
            shift(t_r, t_mv, slice(0, KB), z_expv, 1, z_nb)
            for i in range(KB):
                dve.wait_ge(z_turned, i + 1)
                dve.tensor_copy(h[:, i, 1, :], z_turn_bank[i]).then_inc(z_xnT, 1)
            for i in range(KB):
                dve.wait_ge(z_ffn, i + 1)
                dve.tensor_tensor(x1_block(BATCH - 1, i), z_ffn_bank[i][:], x1_block(BATCH - 1, i), ALU.add
                                  ).then_inc(z_final, 1)

        @block.gpsimd
        def _(pool):
            def u_plus(n):
                pool.wait_ge(u_relu, n + 1)
                pool.wait_ge(u_ln, n + 1)
                pool.tensor_tensor(ut_of(n), ur[:], ut_of(n), ALU.add).then_inc(u_arg, 1)

            def u_times(n):
                pool.wait_ge(u_sig, n + 1)
                if n >= 2 * KB:
                    pool.wait_ge(y_init, n - 2 * KB + 1)
                pool.tensor_tensor(u[:, n // KB % 2, n % KB, :], acc_of(n), ut_of(n), ALU.mult).then_inc(u_done, 1)

            def g_times(n):
                pool.wait_ge(g_sig, n - 2)
                pool.tensor_tensor(gate[:, n % KB, :], gate[:, n % KB, :], gt[:, n % 2, :], ALU.mult).then_inc(g_done, 1)

            def dt_times_u(n, k):
                pool.wait_ge(d_dt, n + 1)
                pool.wait_ge(u_done, n + 1)
                pool.tensor_tensor(dtu[:, k % 2, :], dt[:, k % 2, :], u[:, n // KB % 2, k, :], ALU.mult).then_inc(d_dtu, 1)

            def times_b(b, s, k, j):
                pool.wait_ge(b_landed[j], (b + 1) * 16)
                if s * PAIRS + j >= 2:
                    pool.wait_ge(scanned, s * PAIRS + j - 1)
                pool.tensor_tensor(dbu[:, j % 2], b_rep[:, j],
                                   dtu[:, k % 2, :].unsqueeze(1).to_broadcast([P, 2, L]), ALU.mult).then_inc(mulb, 1)

            def load_factor(r):
                src = factors[r].rearrange("(k p) e -> p k e", p=P)
                if r == 0:
                    pool.dma_start(fsum[:], src).then_inc(f_landed, 16)
                else:
                    pool.wait_ge(f_landed, r * 16)
                    pool.dma_start(fsum[:], src, accum_op=ALU.add).then_inc(f_landed, 16)

            def step(s):
                b, k = divmod(s, KB)
                nu, ng = s + KB + 1, s + KB - 2
                for j in range(PAIRS):
                    if s == 0 and j == 1:
                        u_plus(KB)
                    if s == 0 and j == 3:
                        u_times(KB)
                    if j == 4 and nu < STEPS:
                        u_plus(nu)
                    if j == 7 and nu < STEPS:
                        u_times(nu)
                    if j % 4 == 2 and 2 * s + j // 4 + 1 < FR:
                        load_factor(2 * s + j // 4 + 1)
                    times_b(b, s, k, j)
                if s == 0:
                    pool.wait_ge(f_sig, 1)
                    pool.tensor_tensor(first_gates, first_gates, first_gt, ALU.mult).then_inc(f_done, 1)
                elif ng < STEPS:
                    g_times(ng)
                if s + 1 < STEPS:
                    dt_times_u(s + 1, (k + 1) % KB)

            pool.memset(ident[:], 0.0).then_inc(ident_zero, 1)
            pool.wait_ge(ident_zero, 1)
            pool.affine_select(out=ident[:], in_=ident[:], compare_op=ALU.not_equal, fill=1.0, base=0,
                               pattern=[[-1, P]], channel_multiplier=1).then_inc(ident_ready, 1)
            pool.wait_ge(x_landed, 16)
            load_factor(0)
            u_plus(0)
            for k in range(1, KB):
                u_plus(k)
                u_times(k - 1)
            u_times(KB - 1)
            dt_times_u(0, 0)
            for s in range(STEPS):
                pool.wait_ge(d_dtu, s + 1)
                step(s)


def kernel(**inputs):
    import numpy as np
    import concourse.bacc as bacc
    from concourse.bass_utils import run_bass_kernel_spmd

    a = {n: np.asarray(v) for n, v in inputs.items()}
    f32 = np.float32
    xp = np.zeros((DI, BC_ROW + 2 * N), f32)
    xp[:, 0:RANK] = a["L0_xattn_x_proj_w"].T[:, 0:RANK]
    xp[:, BC_ROW:] = a["L0_xattn_x_proj_w"].T[:, RANK:]
    arrays = {
        "x": a["x"],
        "ctxT": a["ctx_1024"].transpose(2, 0, 1),
        "w_inT": a["L0_xattn_in_proj_w"].T,
        "channel": np.concatenate([a["L0_xattn_conv_w"].reshape(DI, TAPS), a["L0_xattn_conv_b"][:, None],
                                   a["L0_xattn_D"][:, None], a["L0_xattn_A_log"]], axis=1),
        "x_projT": xp,
        "dt_wT": np.concatenate([a["L0_xattn_dt_proj_w"].T, a["L0_xattn_dt_proj_b"][None]]),
        "factors": a["L0_ffn_factors"],
        "bias": a["L0_ffn_bias"].reshape(1, DI),
    }
    arrays = {n: np.ascontiguousarray(v) for n, v in arrays.items()}
    nc = bacc.Bacc("TRN2", target_bir_lowering=False, num_devices=1)
    args = [nc.dram_tensor(n, v.shape, mybir.dt.from_np(v.dtype), kind="ExternalInput").ap()
            for n, v in arrays.items()]
    out = nc.dram_tensor("out", (BATCH, L, DI), F32, kind="ExternalOutput").ap()
    build(nc, *args, out)
    r = run_bass_kernel_spmd(nc, [arrays], core_ids=[0])
    return r.results[0]["out"]
```

```python
from contextlib import ExitStack

import concourse.bass as bass
from concourse import mybir

ALU = mybir.AluOpType
ACT = mybir.ActivationFunctionType
F32 = mybir.dt.float32
BF16 = mybir.dt.bfloat16

P = 128
BATCH, L, DM = 4, 512, 256
DI, N, TAPS, RANK = 512, 16, 4, 16
KB = DI // P
CB = DM // P
FR = 8
PAIRS = N // 2
STEPS = BATCH * KB
EPS = 1e-5
H_RING = 6
BC_ROW = 32
BIAS_ROWS = (0, 64, 96)
WARM_UP = 32
SCALE_SLOTS = (3, 4, 5, 7)
POLY_BELOW = 2.0 ** -7
SQ_SCALE = 3.0 ** -0.5


def build(nc, x, ctxT, w_inT, channel, x_projT, dt_wT, factors, bias, out):
    bc_dram = nc.dram_tensor("bc_scratch", (BATCH, 2 * N, L), F32, kind="Internal").ap()

    with ExitStack() as ctx:
        def sb(name, shape, dt=F32):
            return ctx.enter_context(nc.sbuf_tensor(name, shape, dt))

        def ps(name, shape):
            return ctx.enter_context(nc.psum_tensor(name, shape, F32))

        def sem(name):
            return ctx.enter_context(nc.semaphore(name))

        ident = sb("ident", [P, P])
        diag_d = sb("diag_d", [P, KB, P])
        ones = sb("ones", [P, P], BF16)
        bias_row = sb("bias_row", [P, DI])
        bias_parts = sb("bias_parts", [P, DI], BF16)
        w_in = sb("w_in", [P, CB, DI])
        chan = sb("chan", [P, KB, TAPS + 2 + N])
        cw = chan[:, :, 0:TAPS]
        cb = chan[:, :, TAPS]
        dsk = chan[:, :, TAPS + 1]
        a_log = chan[:, :, TAPS + 2:]
        w_x = sb("w_x", [P, KB, 2 * N + BC_ROW])
        w_dt = sb("w_dt", [P, DI])
        a_neg = sb("a_neg", [P, KB, N])
        fsum = sb("fsum", [P, KB, DI])
        ctx_sb = sb("ctx_sb", [P, CB, L])
        x1 = sb("x1", [P, BATCH * KB * DI])
        b_rep = sb("b_rep", [P, PAIRS, 2, L])
        c_rep = sb("c_rep", [P, PAIRS, 2, L])
        bc = sb("bc", [2 * N + BC_ROW, L])
        dt_low = sb("dt_low", [P, L])
        u = sb("u", [P, 2, KB, L])
        acc = sb("acc", [P, 2, L])
        ut = sb("ut", [P, L])
        gate = sb("gate", [P, KB, L])
        ur = sb("ur", [P, L])
        gt = sb("gt", [P, 2, L])
        g_stat = sb("g_stat", [P, KB, 6])
        g_mv = sb("g_mv", [P, KB, 2])
        g_r = sb("g_r", [P, 3, KB])
        e_dt = sb("e_dt", [P, L])
        l_dt = sb("l_dt", [P, L])
        q_dt = sb("q_dt", [P, L])
        m_dt = sb("m_dt", [P, L], BF16)
        dt = sb("dt", [P, 2, L])
        dtu = sb("dtu", [P, 2, L])
        h = sb("h", [P, H_RING, 2, L])
        yg = sb("yg", [P, L])
        xn = sb("xn", [P, DI])
        xnT = sb("xnT", [P, KB, P])
        t_stat = sb("t_stat", [P, KB, 6])
        t_mv = sb("t_mv", [P, KB, 2])
        t_r = sb("t_r", [P, 3, KB])
        cols = sb("cols", [P, 3])
        eps_col, sq_col, below_col = cols[:, 0:1], cols[:, 1:2], cols[:, 2:3]

        dA = ps("dA", [P, 2, 2, L])
        y = ps("y", [P, L])
        work0 = ps("work0", [P, L])
        work1 = ps("work1", [P, L])
        work2 = ps("work2", [P, L])

        w_x_landed, w_dt_landed, bias_landed, ch_landed = (
            sem(f"{n}_landed") for n in ("w_x", "w_dt", "bias", "ch"))
        w_in_landed = [sem(f"w_in_landed{c}") for c in range(CB)]
        first_ctx_landed = [sem(f"first_ctx_landed{c}") for c in range(CB)]
        ctx_landed = sem("ctx_landed")
        x_landed = sem("x_landed")
        ident_zero = sem("ident_zero")
        ident_ready = sem("ident_ready")
        pads_ready = sem("pads_ready")
        ones_ready = sem("ones_ready")
        bias_rest = sem("bias_rest")
        bias_split = sem("bias_split")
        da_zero = sem("da_zero")
        diag_ready = sem("diag_ready")
        a_exp = sem("a_exp")
        a_ready = sem("a_ready")
        f_landed = sem("f_landed")
        f_scaled = sem("f_scaled")
        in_mm = sem("in_mm")
        tap = sem("tap")
        conv = sem("conv")
        u_abs, u_exp, u_relu, u_ln, u_arg, u_sig, u_done = (
            sem(f"u_{n}") for n in ("abs", "exp", "relu", "ln", "arg", "sig", "done"))
        u_first = sem("u_first")
        mulb_first = sem("mulb_first")
        g_mean, g_var, g_lnv, g_expv, g_nb, g_zn, g_exp, g_ln, g_sig, g_done = (
            sem(f"g_{n}") for n in ("mean", "var", "lnv", "expv", "nb", "zn", "exp", "ln", "sig", "done"))
        f_bn, f_aggr, f_lnv, f_expv, f_nb, f_zn, f_exp, f_ln, f_sig, f_done = (
            sem(f"f_{n}") for n in ("bn", "aggr", "lnv", "expv", "nb", "zn", "exp", "ln", "sig", "done"))
        x_mm = sem("x_mm")
        bc_evac = sem("bc_evac")
        dtl_evac = sem("dtl_evac")
        bc_stored = sem("bc_stored")
        b_landed = [sem(f"b_landed{j}") for j in range(PAIRS)]
        c_landed = [sem(f"c_landed{j}") for j in range(PAIRS)]
        d_mm, d_abs, d_exp, d_ln, d_sq, d_poly, d_mask, d_sel, d_dt, d_dtu = (
            sem(f"d_{n}") for n in ("mm", "abs", "exp", "ln", "sq", "poly", "mask", "sel", "dt", "dtu"))
        y_init = sem("y_init")
        exp_done = sem("exp_done")
        mulb = sem("mulb")
        scanned = sem("scanned")
        mulc = sem("mulc")
        summed = sem("summed")
        gated = sem("gated")
        y_turned = sem("y_turned")
        x1_added = sem("x1_added")
        t_mean, t_var, t_lnv, t_expv, t_nb, t_xn, t_turned, t_xnT, t_ffn, t_final = (
            sem(f"t_{n}") for n in ("mean", "var", "lnv", "expv", "nb", "xn", "turned", "xnT", "ffn", "final"))
        z_bn, z_aggr, z_lnv, z_expv, z_nb, z_xn, z_turned, z_xnT, z_ffn, z_final = (
            sem(f"z_{n}") for n in ("bn", "aggr", "lnv", "expv", "nb", "xn", "turned", "xnT", "ffn", "final"))
        out_stored = sem("out_stored")

        def x1_block(b, k):
            return x1[:, bass.ds(b * (KB * DI) + k * DI, DI)]

        acc_of = lambda n: h[:, n, 0, :] if n < KB else acc[:, n % 2, :]
        ut_of = lambda n: h[:, n, 1, :] if n < KB else yg[:] if n == KB else ut[:]
        first_banks = [work0, work1, work2, y]
        z_turn_bank = [dA[:, i // 2, i % 2, :] for i in range(KB)]
        z_ffn_bank = [work2, work0, work1, y]
        last_xnT = e_dt[:].rearrange("p (k l) -> p k l", k=KB)
        first_gates = [gate[:, i:e, :].rearrange("p k l -> p (k l)") for i, e in ((0, 1), (1, KB - 1))]
        x_last = (BATCH - 1) * KB * DI
        first_gt = [x1[:, x_last + i * L:x_last + e * L] for i, e in ((0, 1), (1, KB - 1))]

        conv_order = [(n, i) for m in range(0, KB + 2, 2) for i in range(1, TAPS) for n in (m, m + 1)]
        conv_order += [(n, i) for n in range(KB + 2, STEPS) for i in range(1, TAPS)]

        def conv_count(n, i=TAPS - 1):
            return conv_order.index((n, i)) + 1

        def x1_columns(b, k):
            return x1[:, bass.ds(b * (KB * DI), KB * DI)].rearrange("p (t d) -> p t d", t=KB)[:, :, k * P:(k + 1) * P]

        block = ctx.enter_context(nc.Block())

        @block.sync
        def _(sp):
            for c in range(CB):
                sp.dma_start(ctx_sb[:, c, :], ctxT[c * P:(c + 1) * P, 0, :]).then_inc(first_ctx_landed[c], 16)
                sp.dma_start(w_in[:, c, :], w_inT[c * P:(c + 1) * P, :]).then_inc(w_in_landed[c], 16)
            sp.dma_start(chan[:], channel.rearrange("(k p) t -> p k t", p=P)).then_inc(ch_landed, 16)
            sp.dma_start(w_x[:], x_projT.rearrange("(k p) e -> p k e", p=P)).then_inc(w_x_landed, 16)
            sp.wait_ge(pads_ready, 1)
            sp.dma_start(w_dt[0:RANK + 1, :], dt_wT).then_inc(w_dt_landed, 16)
            for row in BIAS_ROWS:
                sp.dma_start(bias_row[row:row + 1, :], bias).then_inc(bias_landed, 16)
            sp.dma_start(x1[:, 0:KB * DI].rearrange("p (t d) -> p t d", t=KB),
                         x[0].rearrange("(t p) d -> p t d", p=P)).then_inc(x_landed, 16)
            sp.wait_ge(in_mm, KB)
            sp.dma_start(ctx_sb[:], ctxT[:, 1, :].rearrange("(c p) l -> p c l", p=P)).then_inc(ctx_landed, 16)

            def spread_bc(b):
                sp.wait_ge(bc_evac, b + 1)
                sp.dma_start(bc_dram[bass.ds(b, 1)].rearrange("b n l -> (b n) l"),
                             bc[BC_ROW:BC_ROW + 2 * N, :]).then_inc(bc_stored, 16)
                sp.wait_ge(bc_stored, (b + 1) * 16)
                rows = bc_dram[bass.ds(b, 1)].rearrange("b n l -> b (n l)")
                for j in range(PAIRS + 1):
                    if j < PAIRS:
                        if b > 0:
                            sp.wait_ge(mulb, b * (KB * PAIRS) - PAIRS + j + 1)
                        sp.dma_start(b_rep[:, j].rearrange("p i l -> p (i l)"),
                                     rows[:, 2 * j * L:(2 * j + 2) * L].to_broadcast([P, 2 * L])
                                     ).then_inc(b_landed[j], 16)
                    if j > 0:
                        if b > 0:
                            sp.wait_ge(mulc, b * (KB * PAIRS) - PAIRS + j)
                        sp.dma_start(c_rep[:, j - 1].rearrange("p i l -> p (i l)"),
                                     rows[:, (N + 2 * j - 2) * L:(N + 2 * j) * L].to_broadcast([P, 2 * L])
                                     ).then_inc(c_landed[j - 1], 16)

            def store(b, k):
                if b < BATCH - 1:
                    sp.wait_ge(t_final, b * KB + k + 1)
                else:
                    sp.wait_ge(z_final, k + 1)
                sp.dma_start(out[bass.ds(b, 1), k * P:(k + 1) * P, :].rearrange("b p d -> (b p) d"),
                             x1_block(b, k)).then_inc(out_stored, 16)

            spread_bc(0)
            for b in range(BATCH):
                if b + 1 < BATCH:
                    sp.wait_ge(x_landed, (b + 1) * 16)
                    if b + 2 == BATCH:
                        sp.wait_ge(f_done, len(first_gates))
                    sp.dma_start(x1[:, (b + 1) * KB * DI:(b + 2) * KB * DI].rearrange("p (t d) -> p t d", t=KB),
                                 x[b + 1].rearrange("(t p) d -> p t d", p=P)).then_inc(x_landed, 16)
                if b >= 2:
                    store(b - 2, KB - 1)
                if b >= 1:
                    store(b - 1, 0)
                if b + 2 < BATCH:
                    sp.wait_ge(in_mm, (b + 2) * KB)
                    sp.wait_ge(ctx_landed, (b + 1) * 16)
                    sp.dma_start(ctx_sb[:], ctxT[:, b + 2, :].rearrange("(c p) l -> p c l", p=P)
                                 ).then_inc(ctx_landed, 16)
                if b >= 1:
                    store(b - 1, 1)
                if b + 1 < BATCH:
                    spread_bc(b + 1)
                if b >= 1:
                    store(b - 1, 2)
            store(BATCH - 2, KB - 1)
            for k in range(KB):
                store(BATCH - 1, k)
            sp.wait_ge(out_stored, STEPS * 16)

        @block.tensor
        def _(pe):
            def in_proj(bank, k, first=False):
                for c in range(CB):
                    if first:
                        pe.wait_ge(first_ctx_landed[c], 16)
                        pe.wait_ge(w_in_landed[c], 16)
                    mm = pe.matmul(bank[:], w_in[:, c, k * P:(k + 1) * P], ctx_sb[:, c, :],
                                   start=(c == 0), stop=(c == CB - 1))
                mm.then_inc(in_mm, 1)

            def x_proj(ub, ks):
                for k in ks:
                    mm = pe.matmul(work2[0:2 * N + BC_ROW, :], w_x[:, k, :], u[:, ub % 2, k, :], start=(k == 0),
                                   stop=(k == KB - 1))
                if KB - 1 in ks:
                    mm.then_inc(x_mm, 1)

            def dt_proj(k, bank=work2):
                pe.matmul(bank[:], w_dt[:, k * P:(k + 1) * P], dt_low[:], start=True, stop=True).then_inc(d_mm, 1)

            def turn_y(s):
                pe.wait_ge(gated, s + 1)
                for t in range(KB):
                    tr = pe.transpose(work0[:, t * P:(t + 1) * P], yg[:, t * P:(t + 1) * P], ident[:])
                tr.then_inc(y_turned, 1)

            def turn_xn(t, bank=work1):
                pe.wait_ge(t_xn, t + 1)
                for k in range(KB):
                    tr = pe.transpose(bank[:, k * P:(k + 1) * P], xn[:, k * P:(k + 1) * P], ident[:])
                tr.then_inc(t_turned, 1)

            def turn_z(i):
                pe.wait_ge(z_xn, i + 1)
                for k in range(KB):
                    tr = pe.transpose(z_turn_bank[i][:, k * P:(k + 1) * P], h[:, i, 0, k * P:(k + 1) * P], ident[:])
                tr.then_inc(z_turned, 1)

            def last_layer(t, half, xnT=xnT[:]):
                if half == 0:
                    pe.wait_ge(t_xnT, t + 1)
                for k in (0, 1) if half == 0 else (2, 3):
                    pe.matmul(work1[:], xnT[:, k, :], fsum[:, k, :], start=(k == 0), stop=False)
                if half == 1:
                    pe.matmul(work1[:], ones[:], bias_parts[:], start=False, stop=False)
                    pe.matmul(work1[:], ident[:], x1_block(t // KB, t % KB), start=False, stop=True).then_inc(t_ffn, 1)

            def state_sum(s, j):
                pe.wait_ge(mulc, s * PAIRS + j + 1)
                for i in range(2):
                    mm = pe.matmul(y[:], ident[:], h[:, (s * PAIRS + j) % H_RING, i, :], start=False,
                                   stop=(j == PAIRS - 1 and i == 1))
                mm.then_inc(summed, 1)

            def step(s):
                b, k = divmod(s, KB)
                nu, nt = s + KB + 2, s - KB
                turns = k == KB - 1 and b + 1 < BATCH
                if s + 1 < STEPS and not turns:
                    pe.wait_ge(d_dt, s + 1)
                    dt_proj(k + 1)
                if nt >= 1:
                    if nt >= 2:
                        pe.wait_ge(t_final, nt - 1)
                    turn_xn(nt - 1)
                if turns:
                    pe.wait_ge(d_dt, s + 1)
                    pe.wait_ge(u_done, s + KB + 1)
                    x_proj(b + 1, range(KB))
                pe.wait_ge(u_done, s + 1)
                if s > 0:
                    pe.wait_ge(gated, s)
                else:
                    pe.wait_ge(d_dt, 1)
                pe.matmul(y[:], diag_d[:, k, :], u[:, b % 2, k, :], start=True, stop=False).then_inc(y_init, 1)
                if s > 0:
                    pe.wait_ge(conv, conv_count(min(s + KB + 1, STEPS - 1)))
                    turn_y(s - 1)
                for j in range(PAIRS):
                    state_sum(s, j)
                    if j == 1:
                        if turns:
                            pe.wait_ge(bc_evac, b + 2)
                            pe.wait_ge(dtl_evac, b + 2)
                            dt_proj(0)
                    if j == 2 and nt >= 1:
                        last_layer(nt - 1, 0)
                    if j == (3 if s > 0 else 0) and nu < STEPS:
                        pe.wait_ge(ctx_landed, nu // KB * 16)
                        if s > 0:
                            pe.wait_ge(x1_added, s)
                        else:
                            pe.wait_ge(conv, conv_count(KB))
                        in_proj(work0, nu % KB)
                    if j == 4 and nt >= 1 and s < STEPS - 1:
                        last_layer(nt - 1, 1)
            pe.wait_ge(ones_ready, 1)
            for _ in range(WARM_UP):
                pe.matmul(y[:, 0:P], ones[:], ones[:], start=True, stop=True)
            for k in range(KB):
                in_proj(first_banks[k], k, first=(k == 0))
            pe.wait_ge(ctx_landed, 16)
            pe.wait_ge(conv, conv_count(0))
            in_proj(work0, 0)
            pe.wait_ge(conv, conv_count(1))
            in_proj(work1, 1)
            pe.wait_ge(w_x_landed, 16)
            pe.wait_ge(pads_ready, 1)
            pe.wait_ge(conv, conv_count(2))
            for k in range(KB):
                if k < KB // 2:
                    pe.wait_ge(u_done, k + 1)
                else:
                    pe.wait_ge(u_first, k - KB // 2 + 1)
                x_proj(0, [k])
            pe.wait_ge(w_dt_landed, 16)
            pe.wait_ge(conv, conv_count(KB - 1))
            pe.wait_ge(dtl_evac, 1)
            dt_proj(0, y)
            pe.wait_ge(bc_evac, 1)
            pe.wait_ge(ident_ready, 1)
            pe.wait_ge(diag_ready, KB)
            for s in range(STEPS):
                if s == KB + 1:
                    pe.wait_ge(f_scaled, KB)
                    pe.wait_ge(bias_split, 3)
                step(s)
            turn_y(STEPS - 1)
            turn_xn(STEPS - KB - 1, work2)
            last_layer(STEPS - KB - 2, 1)
            pe.wait_ge(t_final, STEPS - KB - 1)
            last_layer(STEPS - KB - 1, 0, last_xnT)
            pe.wait_ge(scanned, STEPS * PAIRS)
            turn_z(0)
            last_layer(STEPS - KB - 1, 1, last_xnT)
            pe.wait_ge(x1_added, STEPS)
            for i in range(1, KB + 1):
                if i < KB:
                    turn_z(i)
                pe.wait_ge(z_xnT, i)
                if z_ffn_bank[i - 1] is work1:
                    pe.wait_ge(t_final, STEPS - KB)
                for k in range(KB):
                    pe.matmul(z_ffn_bank[i - 1][:], h[:, i - 1, 1, k * P:(k + 1) * P], fsum[:, k, :],
                              start=(k == 0), stop=False)
                pe.matmul(z_ffn_bank[i - 1][:], ones[:], bias_parts[:], start=False, stop=True).then_inc(z_ffn, 1)

        @block.scalar
        def _(act):
            def conv_tap(bank, n, k):
                act.wait_ge(in_mm, n + 1)
                if n >= KB + 2:
                    act.wait_ge(u_done, n - 1)
                act.activation(acc_of(n), bank[:], ACT.Identity, bias=cb[:, k:k + 1],
                               scale=cw[:, k, TAPS - 1:TAPS]).then_inc(tap, 1)

            def u_abs_(n):
                act.wait_ge(conv, conv_count(n))
                if n > KB + 1:
                    act.wait_ge(u_done, n)
                act.activation(ut_of(n), acc_of(n), ACT.Abs).then_inc(u_abs, 1)

            def u_exp_(n):
                act.wait_ge(u_abs, n + 1)
                act.activation(ut_of(n), ut_of(n), ACT.Exp, scale=-1.0).then_inc(u_exp, 1)

            def u_relu_(n):
                act.wait_ge(u_arg, n)
                act.activation(ur[:], acc_of(n), ACT.Relu, scale=-1.0).then_inc(u_relu, 1)

            def u_ln_(n):
                act.wait_ge(u_exp, n + 1)
                act.activation(ut_of(n), ut_of(n), ACT.Ln, bias=1.0).then_inc(u_ln, 1)

            def u_sig_(n):
                act.wait_ge(u_arg, n + 1)
                act.activation(ut_of(n), ut_of(n), ACT.Exp, scale=1.0 if n < KB else -1.0).then_inc(u_sig, 1)

            def minus_mean(mv, b, k, scratch, done):
                act.activation(scratch, x1_block(b, k), ACT.Copy, scale=-1.0 / DI, accum_out=mv[:, k, 0:1]
                               ).then_inc(done, 1)

            def var_sum(mv, b, k, scratch, after, n, done):
                act.wait_ge(after, n)
                act.activation(scratch, x1_block(b, k), ACT.Square, bias=mv[:, k, 0:1], accum_out=mv[:, k, 1:2]
                               ).then_inc(done, 1)

            def lnv(r, mv, ks, after, n, done, scale=1.0):
                act.wait_ge(after, n)
                act.activation(r[:, 0, ks], mv[:, ks, 1], ACT.Ln, bias=eps_col, scale=scale).then_inc(done, 1)

            def nb(r, mv, k, after, n, done):
                act.wait_ge(after, n)
                act.activation(r[:, 2, k:k + 1], mv[:, k, 0:1], ACT.Identity, scale=r[:, 1, k:k + 1]
                               ).then_inc(done, 1)

            def expv(r, ks, after, n, done):
                act.wait_ge(after, n)
                act.activation(r[:, 1, ks], r[:, 0, ks], ACT.Exp, scale=-0.5).then_inc(done, 1)

            def norm(dst, b, k, r, done):
                act.activation(dst, x1_block(b, k), ACT.Identity, bias=r[:, 2, k:k + 1],
                               scale=r[:, 1, k:k + 1]).then_inc(done, 1)

            def g_zn_(n):
                if n >= KB:
                    act.wait_ge(gated, n - KB + 1)
                act.wait_ge(g_nb, n - 2)
                norm(gate[:, n % KB, :], n // KB, n % KB, g_r, g_zn)

            def g_exp_(n):
                act.wait_ge(g_zn, n - 2)
                act.activation(gt[:, n % 2, :], gate[:, n % KB, :], ACT.Exp, scale=-1.0).then_inc(g_exp, 1)

            def g_ln_(n):
                act.wait_ge(g_exp, n - 2)
                act.activation(gt[:, n % 2, :], gt[:, n % 2, :], ACT.Ln, bias=1.0).then_inc(g_ln, 1)

            def g_sig_(n):
                act.wait_ge(g_ln, n - 2)
                act.activation(gt[:, n % 2, :], gt[:, n % 2, :], ACT.Exp, scale=-1.0).then_inc(g_sig, 1)

            def x_evac(b):
                act.wait_ge(x_mm, b + 1)
                if b > 0:
                    act.wait_ge(bc_stored, b * 16)
                    act.wait_ge(d_mm, b * KB)
                act.activation(bc[BC_ROW:BC_ROW + 2 * N, :], work2[BC_ROW:BC_ROW + 2 * N, :], ACT.Copy
                               ).then_inc(bc_evac, 1)
                act.activation(dt_low[0:RANK, :], work2[0:RANK, :], ACT.Copy).then_inc(dtl_evac, 1)

            def d_abs_(n):
                act.wait_ge(d_mm, n + 1)
                if n > 0:
                    act.wait_ge(d_dt, n)
                act.activation(e_dt[:], (y if n == 0 else work2)[:], ACT.Abs).then_inc(d_abs, 1)

            def d_exp_(n):
                act.wait_ge(d_abs, n + 1)
                act.activation(e_dt[:], e_dt[:], ACT.Exp, scale=-1.0).then_inc(d_exp, 1)

            def d_ln_(n):
                act.activation(l_dt[:], e_dt[:], ACT.Ln, bias=1.0).then_inc(d_ln, 1)

            def d_sq_(n):
                act.wait_ge(d_exp, n + 1)
                act.activation(q_dt[:], e_dt[:], ACT.Square, scale=SQ_SCALE, bias=sq_col).then_inc(d_sq, 1)

            def d_mask_(n):
                act.activation(m_dt[:], e_dt[:], ACT.Relu, bias=below_col).then_inc(d_mask, 1)

            def t_xn_(t):
                act.wait_ge(t_nb, t + 1)
                norm(xn[:], t // KB, t % KB, t_r, t_xn)

            def t_xnT_(t):
                act.wait_ge(t_turned, t + 1)
                if t > 0:
                    act.wait_ge(t_ffn, t)
                act.activation(xnT[:].rearrange("p k l -> p (k l)"), work1[:], ACT.Copy).then_inc(t_xnT, 1)

            def t_final_(t):
                act.wait_ge(t_ffn, t + 1)
                act.activation(x1_block(t // KB, t % KB), work1[:], ACT.Copy).then_inc(t_final, 1)

            def decay(s, k, j, i):
                act.activation(dA[:, j % 2, i, 1:L], dt[:, k % 2, 1:L], ACT.Exp,
                               scale=a_neg[:, k, 2 * j + i:2 * j + i + 1]).then_inc(exp_done, 1)

            def step(s):
                b, k = divmod(s, KB)
                nu, ng, nt = s + KB + 1, s + KB - 1, s - KB
                is_u, is_g, is_t, is_d = nu < STEPS, ng < STEPS, nt >= 0, s + 1 < STEPS
                gb, gk = divmod(ng, KB)
                late = k == KB - 1 and is_d or 0 < s < STEPS - KB - 1
                for j in range(PAIRS):
                    if j == 1 and is_g:
                        var_sum(g_mv, gb, gk, gt[:, ng % 2, :], g_mean, ng - 2, g_var)
                    if j == 2:
                        if s == 0:
                            u_sig_(KB)
                        if is_u:
                            u_abs_(nu)
                    if j == 3:
                        if is_u:
                            u_relu_(nu)
                            u_ln_(nu)
                        if is_g:
                            nb(g_r, g_mv, gk, g_expv, ng - 2, g_nb)
                    if j == 5:
                        if is_t and late:
                            var_sum(t_mv, b - 1, k, xn[:], t_mean, nt + 1, t_var)
                        if is_d and late:
                            d_abs_(s + 1)
                        elif is_d:
                            d_sq_(s + 1)
                            d_ln_(s + 1)
                    if j == 6:
                        if is_d and late:
                            d_sq_(s + 1)
                            d_ln_(s + 1)
                            d_mask_(s + 1)
                        if is_t and late:
                            expv(t_r, slice(k, k + 1), t_lnv, nt + 1, t_expv)
                        elif is_t:
                            var_sum(t_mv, b - 1, k, xn[:], t_mean, nt + 1, t_var)
                    if j == 7:
                        if is_t and not late:
                            expv(t_r, slice(k, k + 1), t_lnv, nt + 1, t_expv)
                        if is_g:
                            g_zn_(ng)
                    if j == 4 and is_d and not late:
                        d_abs_(s + 1)
                    if s * PAIRS + j >= 2:
                        act.wait_ge(scanned, s * PAIRS + j - 1)
                    decay(s, k, j, 0)
                    if j == 0 and nt >= 2:
                        t_final_(nt - 2)
                    if j == 0 and is_g:
                        act.wait_ge(x_landed, (gb + 1) * 16)
                        if ng >= 5:
                            act.wait_ge(g_done, ng - 4)
                        minus_mean(g_mv, gb, gk, gt[:, ng % 2, :], g_mean)
                    if j == 1 and is_g:
                        lnv(g_r, g_mv, slice(gk, gk + 1), g_var, ng - 2, g_lnv, 1.0 / DI)
                    if j == 2:
                        if is_u:
                            u_exp_(nu)
                        if is_g:
                            expv(g_r, slice(gk, gk + 1), g_lnv, ng - 2, g_expv)
                    if j == 3 and k == KB - 1 and is_d:
                        x_evac(b + 1)
                    if j == 3 and nt >= 1:
                        t_xnT_(nt - 1)
                    if j == 4 and is_u:
                        u_sig_(nu)
                    if j == 4 and is_d and not late:
                        d_exp_(s + 1)
                    if j == 4 and is_t:
                        act.wait_ge(x1_added, (nt // KB + 1) * KB)
                        if nt > 0:
                            act.wait_ge(t_turned, nt)
                        minus_mean(t_mv, b - 1, k, xn[:], t_mean)
                    if j == 5:
                        if is_d and late:
                            d_exp_(s + 1)
                        elif is_d:
                            d_mask_(s + 1)
                        if is_t and late:
                            lnv(t_r, t_mv, slice(k, k + 1), t_var, nt + 1, t_lnv, 1.0 / DI)
                    if j == 6 and is_t and not late:
                        lnv(t_r, t_mv, slice(k, k + 1), t_var, nt + 1, t_lnv, 1.0 / DI)
                    if j == 7 and is_t:
                        nb(t_r, t_mv, k, t_expv, nt + 1, t_nb)
                    if j == 7:
                        if nu + 1 < STEPS:
                            conv_tap(work0, nu + 1, (nu + 1) % KB)
                        if is_g:
                            g_exp_(ng)
                    decay(s, k, j, 1)
                    if s < len(first_gates):
                        if j == 0:
                            act.wait_ge(f_zn, KB - 1)
                            act.activation(first_gt[s], first_gates[s], ACT.Exp, scale=-1.0).then_inc(f_exp, 1)
                        if j == 2:
                            act.wait_ge(f_exp, s + 1)
                            act.activation(first_gt[s], first_gt[s], ACT.Ln, bias=1.0).then_inc(f_ln, 1)
                        if j == 4:
                            act.wait_ge(f_ln, s + 1)
                            act.activation(first_gt[s], first_gt[s], ACT.Exp, scale=-1.0).then_inc(f_sig, 1)
                    if s == KB - 1 and j in SCALE_SLOTS:
                        if j == SCALE_SLOTS[0]:
                            act.wait_ge(f_landed, FR * 16)
                        i = SCALE_SLOTS.index(j)
                        act.activation(fsum[:, i, :], fsum[:, i, :], ACT.Copy, scale=FR ** -0.5).then_inc(f_scaled, 1)
                if is_g:
                    g_ln_(ng)
                    g_sig_(ng)
                if is_t:
                    t_xn_(nt)

            act.preload_act_table_set("natural_log_exp_and_others")
            act.wait_ge(ch_landed, 16)
            act.wait_ge(pads_ready, 1)
            for k in range(KB):
                conv_tap(first_banks[k], k, k)
            for pair in ((0, 1), (2, 3)):
                for op in (u_abs_, u_exp_, u_ln_, u_sig_):
                    if op == u_sig_ and pair[0] > 0:
                        lnv(g_r, g_mv, slice(0, KB - 1), f_aggr, KB - 1, f_lnv)
                        expv(g_r, slice(0, KB - 1), f_lnv, 1, f_expv)
                        conv_tap(work0, KB, 0)
                    for k in pair:
                        op(k)
                if pair[0] == 0:
                    act.activation(a_neg[:], a_log, ACT.Exp).then_inc(a_exp, 1)
                    act.wait_ge(a_exp, 1)
                    act.activation(a_neg[:], a_neg[:], ACT.Copy, scale=-1.0).then_inc(a_ready, 1)
            conv_tap(work1, KB + 1, 1)
            act.wait_ge(f_nb, 1)
            norm(gate[:, 0, :], 0, 0, g_r, f_zn)
            norm(gate[:, 1, :], 0, 1, g_r, f_zn)
            x_evac(0)
            norm(gate[:, 2, :], 0, 2, g_r, f_zn)
            d_abs_(0)
            d_exp_(0)
            d_sq_(0)
            d_ln_(0)
            d_mask_(0)
            u_abs_(KB)
            u_exp_(KB)
            u_relu_(KB)
            u_ln_(KB)
            act.wait_ge(a_ready, 1)
            act.wait_ge(da_zero, 1)
            for s in range(STEPS):
                act.wait_ge(d_dt, s + 1)
                step(s)
            act.wait_ge(t_turned, STEPS - KB)
            act.activation(e_dt[:], work2[:], ACT.Copy).then_inc(t_xnT, 1)
            for i in range(KB):
                lnv(t_r, t_mv, slice(i, i + 1), z_aggr, i + 1, z_lnv)
                expv(t_r, slice(i, i + 1), z_lnv, i + 1, z_expv)
                if i == 0:
                    t_final_(STEPS - KB - 2)
                act.wait_ge(z_nb, i + 1)
                if i == 0:
                    act.wait_ge(summed, STEPS * PAIRS)
                norm(h[:, i, 0, :], BATCH - 1, i, t_r, z_xn)
            t_final_(STEPS - KB - 1)

        @block.vector
        def _(dve):
            def conv_part(bank, n, k, i):
                if i == 1:
                    dve.wait_ge(tap, n + 1)
                else:
                    dve.wait_ge(conv, conv_count(n, i - 1))
                dve.scalar_tensor_tensor(out=acc_of(n)[:, i:L], in0=bank[:, 0:L - i],
                                         scalar=cw[:, k, TAPS - 1 - i:TAPS - i], in1=acc_of(n)[:, i:L],
                                         op0=ALU.mult, op1=ALU.add).then_inc(conv, 1)

            def split_bias(i, part):
                rows = slice(BIAS_ROWS[i], P)
                if part == 0:
                    if i == 0:
                        dve.wait_ge(bias_landed, 16 * len(BIAS_ROWS))
                    else:
                        dve.wait_ge(bias_rest, i)
                    dve.tensor_copy(bias_parts[rows, :], bias_row[rows, :]).then_inc(bias_split, 1)
                else:
                    dve.wait_ge(bias_split, i)
                    dve.tensor_tensor(bias_row[rows, :], bias_row[rows, :], bias_parts[rows, :], ALU.subtract
                                      ).then_inc(bias_rest, 1)

            def first_arg(n):
                dve.wait_ge(u_ln, n + 1)
                dve.scalar_tensor_tensor(out=ut_of(n), in0=acc_of(n), scalar=0.0, in1=ut_of(n),
                                         op0=ALU.min, op1=ALU.subtract).then_inc(u_arg, 1)

            def stats(stat, b, k, done):
                dve.bn_stats(stat[:, k, :], x1_block(b, k)).then_inc(done, 1)

            def aggr(mv, stat, k, after, n, done):
                dve.wait_ge(after, n)
                dve.bn_aggr(mv[:, k, :], stat[:, k, :]).then_inc(done, 1)

            def shift(r, mv, ks, after, n, done):
                dve.wait_ge(after, n)
                dve.scalar_tensor_tensor(out=r[:, 2, ks], in0=mv[:, ks, 0], scalar=-1.0, in1=r[:, 1, ks],
                                         op0=ALU.mult, op1=ALU.mult).then_inc(done, 1)

            def softplus_parts(n):
                dve.wait_ge(d_sq, n + 1)
                dve.scalar_tensor_tensor(out=q_dt[:], in0=q_dt[:], scalar=13.0 / 16.0, in1=e_dt[:],
                                         op0=ALU.add, op1=ALU.mult).then_inc(d_poly, 1)

            def softplus_select(n):
                dve.wait_ge(d_ln, n + 1)
                dve.wait_ge(d_mask, n + 1)
                dve.wait_ge(d_poly, n + 1)
                dve.copy_predicated(q_dt[:], m_dt[:].bitcast(mybir.dt.uint16), l_dt[:]).then_inc(d_sel, 1)

            def softplus_sum(n):
                dve.wait_ge(d_sel, n + 1)
                if n >= 2:
                    dve.wait_ge(exp_done, (n - 1) * (2 * PAIRS))
                    dve.wait_ge(d_dtu, n - 1)
                dve.scalar_tensor_tensor(out=dt[:, n % 2, :], in0=(y if n == 0 else work2)[:], scalar=0.0,
                                         in1=q_dt[:],
                                         op0=ALU.max, op1=ALU.add).then_inc(d_dt, 1)

            def scan(s, j):
                dve.wait_ge(exp_done, (s * PAIRS + j) * 2 + 2)
                if s * PAIRS + j == 0:
                    dve.wait_ge(mulb_first, 1)
                else:
                    dve.wait_ge(mulb, s * PAIRS + j + 1)
                pair = h[:, (s * PAIRS + j) % H_RING]
                dve.tensor_tensor_scan(pair.rearrange("p i l -> p (i l)"),
                                       dA[:, j % 2].rearrange("p i l -> p (i l)"),
                                       pair.rearrange("p i l -> p (i l)"), 0.0, ALU.mult, ALU.add
                                       ).then_inc(scanned, 1)

            def times_c(b, s, j):
                dve.wait_ge(scanned, s * PAIRS + j + 1)
                dve.wait_ge(c_landed[j], (b + 1) * 16)
                pair = h[:, (s * PAIRS + j) % H_RING]
                dve.tensor_tensor(pair, pair, c_rep[:, j], ALU.mult).then_inc(mulc, 1)

            def gate_y(s):
                dve.wait_ge(summed, (s + 1) * PAIRS)
                if s == 0:
                    dve.wait_ge(u_done, KB + 1)
                if s < KB - 1:
                    dve.wait_ge(f_done, min(s + 1, len(first_gates)))
                else:
                    dve.wait_ge(g_done, s - KB + 2)
                if s > 0:
                    dve.wait_ge(y_turned, s)
                dve.tensor_tensor(yg[:], y[:], gate[:, s % KB, :], ALU.mult).then_inc(gated, 1)

            def add_x1(s):
                b, k = divmod(s, KB)
                dve.wait_ge(y_turned, s + 1)
                dve.wait_ge(g_zn, b * KB + 1)
                dve.tensor_tensor(x1_columns(b, k), work0[:].rearrange("p (t d) -> p t d", t=KB),
                                  x1_columns(b, k), ALU.add).then_inc(x1_added, 1)

            def step(s):
                b, k = divmod(s, KB)
                nv = s + KB + 2
                is_c, is_d = nv < STEPS, s + 1 < STEPS
                for j in range(PAIRS):
                    if j == 3 and s > 0:
                        add_x1(s - 1)
                    if j == 6 and is_d:
                        softplus_select(s + 1)
                    scan(s, j)
                    if j == 4 and s < len(first_gates):
                        dve.wait_ge(f_sig, s + 1)
                        dve.tensor_tensor(first_gates[s], first_gates[s], first_gt[s], ALU.mult).then_inc(f_done, 1)
                    if j == 0 and s > 0 and nv - 1 < STEPS:
                        conv_part(work0, nv - 1, (nv - 1) % KB, 3)
                    if s == 0 and j <= 2 * (len(BIAS_ROWS) - 1):
                        split_bias((j + 1) // 2, j % 2)
                    if j == 1 and s > 0:
                        gate_y(s - 1)
                    if j == 5 and is_d:
                        softplus_parts(s + 1)
                    if j == 6 and is_d:
                        softplus_sum(s + 1)
                    if j == 7 and is_c:
                        conv_part(work0, nv, nv % KB, 1)
                    if j > 0:
                        times_c(b, s, j - 1)
                if is_c:
                    conv_part(work0, nv, nv % KB, 2)
                times_c(b, s, PAIRS - 1)

            dve.memset(ones[:], 1.0).then_inc(ones_ready, 1)
            dve.memset(eps_col, EPS)
            dve.memset(sq_col, -0.75 * SQ_SCALE)
            dve.memset(below_col, -POLY_BELOW)
            dve.memset(w_dt[:], 0.0)
            dve.memset(bias_row[:], 0.0)
            dve.memset(dt_low[:], 1.0).then_inc(pads_ready, 1)
            dve.memset(dA[:, :, :, 0:1], 0.0).then_inc(da_zero, 1)
            def first_taps(blocks, i):
                for n in blocks:
                    conv_part(first_banks[n % KB], n, n % KB, i)

            def first_times(n):
                dve.wait_ge(u_sig, n + 1)
                dve.tensor_tensor(u[:, 0, n, :], acc_of(n), ut_of(n), ALU.mult).then_inc(u_first, 1)

            for i in range(1, TAPS):
                first_taps((0, 1), i)
            first_taps((2, 3), 1)
            first_taps((2, 3), 2)
            first_arg(0)
            first_arg(1)
            first_taps((2, 3), 3)
            dve.wait_ge(ident_ready, 1)
            dve.wait_ge(ch_landed, 16)
            for k in range(KB):
                dve.tensor_scalar(diag_d[:, k, :], ident[:], dsk[:, k:k + 1], None, ALU.mult).then_inc(diag_ready, 1)
            dve.wait_ge(x_landed, 16)
            for k in range(KB - 1):
                stats(g_stat, 0, k, f_bn)
            for k in range(KB - 1):
                aggr(g_mv, g_stat, k, f_bn, k + 1, f_aggr)
            first_arg(2)
            first_arg(3)
            shift(g_r, g_mv, slice(0, KB - 1), f_expv, 1, f_nb)
            first_times(2)
            first_times(3)
            for i in range(1, TAPS):
                first_taps((KB, KB + 1), i)
            softplus_parts(0)
            softplus_select(0)
            softplus_sum(0)
            dve.wait_ge(d_dt, 1)
            dve.wait_ge(u_done, 1)
            dve.tensor_tensor(dtu[:, 0, :], dt[:, 0, :], u[:, 0, 0, :], ALU.mult).then_inc(d_dtu, 1)
            dve.wait_ge(d_dtu, 1)
            dve.wait_ge(b_landed[0], 16)
            dve.tensor_tensor(h[:, 0], b_rep[:, 0], dtu[:, 0, :].unsqueeze(1).to_broadcast([P, 2, L]), ALU.mult
                              ).then_inc(mulb_first, 1)
            for s in range(STEPS):
                step(s)
            gate_y(STEPS - 1)
            add_x1(STEPS - 1)
            dve.wait_ge(x1_added, STEPS)
            for i in range(KB):
                stats(t_stat, BATCH - 1, i, z_bn)
                aggr(t_mv, t_stat, i, z_bn, i + 1, z_aggr)
                if i > 0:
                    shift(t_r, t_mv, slice(i - 1, i), z_expv, i, z_nb)
            for i in range(KB):
                if i == 1:
                    shift(t_r, t_mv, slice(KB - 1, KB), z_expv, KB, z_nb)
                dve.wait_ge(z_turned, i + 1)
                dve.tensor_copy(h[:, i, 1, :], z_turn_bank[i]).then_inc(z_xnT, 1)
            for i in range(KB):
                dve.wait_ge(z_ffn, i + 1)
                dve.tensor_tensor(x1_block(BATCH - 1, i), z_ffn_bank[i][:], x1_block(BATCH - 1, i), ALU.add
                                  ).then_inc(z_final, 1)

        @block.gpsimd
        def _(pool):
            def u_plus(n):
                pool.wait_ge(u_relu, n - KB + 1)
                pool.wait_ge(u_ln, n + 1)
                pool.tensor_tensor(ut_of(n), ur[:], ut_of(n), ALU.add).then_inc(u_arg, 1)

            def u_times(n):
                pool.wait_ge(u_sig, n + 1)
                if n >= 2 * KB:
                    pool.wait_ge(y_init, n - 2 * KB + 1)
                pool.tensor_tensor(u[:, n // KB % 2, n % KB, :], acc_of(n), ut_of(n), ALU.mult
                                   ).then_inc(u_done, 1 if n != KB else 1 + KB // 2)

            def g_times(n):
                pool.wait_ge(g_sig, n - 2)
                pool.tensor_tensor(gate[:, n % KB, :], gate[:, n % KB, :], gt[:, n % 2, :], ALU.mult).then_inc(g_done, 1)

            def dt_times_u(n, k):
                pool.wait_ge(d_dt, n + 1)
                pool.wait_ge(u_done, n + 1)
                pool.tensor_tensor(dtu[:, k % 2, :], dt[:, k % 2, :], u[:, n // KB % 2, k, :], ALU.mult).then_inc(d_dtu, 1)

            def times_b(b, s, k, j):
                pool.wait_ge(b_landed[j], (b + 1) * 16)
                if s * PAIRS + j >= H_RING:
                    pool.wait_ge(summed, s * PAIRS + j + 1 - H_RING)
                pool.tensor_tensor(h[:, (s * PAIRS + j) % H_RING], b_rep[:, j],
                                   dtu[:, k % 2, :].unsqueeze(1).to_broadcast([P, 2, L]), ALU.mult
                                   ).then_inc(mulb, 2 if s == 0 and j == 1 else 1)

            def load_factor(r):
                src = factors[r].rearrange("(k p) e -> p k e", p=P)
                if r == 0:
                    pool.dma_start(fsum[:], src).then_inc(f_landed, 16)
                else:
                    pool.wait_ge(f_landed, r * 16)
                    pool.dma_start(fsum[:], src, accum_op=ALU.add).then_inc(f_landed, 16)

            def step(s):
                b, k = divmod(s, KB)
                nu, ng = s + KB + 1, s + KB - 2
                for j in range(PAIRS):
                    if s == 0 and j == 1:
                        u_plus(KB)
                    if s == 0 and j == 3:
                        u_times(KB)
                    if j == 4 and nu < STEPS:
                        u_plus(nu)
                    if j == 7 and nu < STEPS:
                        u_times(nu)
                    if j % 4 == 1 and s > 0 and 3 + 2 * (s - 1) + j // 4 < FR:
                        load_factor(3 + 2 * (s - 1) + j // 4)
                    if s > 0 or j > 0:
                        times_b(b, s, k, j)
                if s > 0 and ng < STEPS:
                    g_times(ng)
                if s + 1 < STEPS:
                    dt_times_u(s + 1, (k + 1) % KB)

            pool.memset(ident[:], 0.0).then_inc(ident_zero, 1)
            pool.wait_ge(ident_zero, 1)
            pool.affine_select(out=ident[:], in_=ident[:], compare_op=ALU.not_equal, fill=1.0, base=0,
                               pattern=[[-1, P]], channel_multiplier=1).then_inc(ident_ready, 1)
            pool.wait_ge(x_landed, 16)
            load_factor(0)
            load_factor(1)
            for k in range(KB // 2):
                u_times(k)
            load_factor(2)
            for s in range(STEPS):
                pool.wait_ge(d_dtu, s + 1)
                step(s)


def kernel(**inputs):
    import numpy as np
    import concourse.bacc as bacc
    from concourse.bass_utils import run_bass_kernel_spmd

    a = {n: np.asarray(v) for n, v in inputs.items()}
    f32 = np.float32
    xp = np.zeros((DI, BC_ROW + 2 * N), f32)
    xp[:, 0:RANK] = a["L0_xattn_x_proj_w"].T[:, 0:RANK]
    xp[:, BC_ROW:] = a["L0_xattn_x_proj_w"].T[:, RANK:]
    arrays = {
        "x": a["x"],
        "ctxT": a["ctx_1024"].transpose(2, 0, 1),
        "w_inT": a["L0_xattn_in_proj_w"].T,
        "channel": np.concatenate([a["L0_xattn_conv_w"].reshape(DI, TAPS), a["L0_xattn_conv_b"][:, None],
                                   a["L0_xattn_D"][:, None], a["L0_xattn_A_log"]], axis=1),
        "x_projT": xp,
        "dt_wT": np.concatenate([a["L0_xattn_dt_proj_w"].T, a["L0_xattn_dt_proj_b"][None]]),
        "factors": a["L0_ffn_factors"],
        "bias": a["L0_ffn_bias"].reshape(1, DI),
    }
    arrays = {n: np.ascontiguousarray(v) for n, v in arrays.items()}
    nc = bacc.Bacc("TRN2", target_bir_lowering=False, num_devices=1)
    args = [nc.dram_tensor(n, v.shape, mybir.dt.from_np(v.dtype), kind="ExternalInput").ap()
            for n, v in arrays.items()]
    out = nc.dram_tensor("out", (BATCH, L, DI), F32, kind="ExternalOutput").ap()
    build(nc, *args, out)
    r = run_bass_kernel_spmd(nc, [arrays], core_ids=[0])
    return r.results[0]["out"]
```
